# Optimizing a Trainium2 kernel written in Bass

```python
import numpy as np
import jax
import jax.numpy as jnp

def _softmax(x, axis=-1):
    return jax.nn.softmax(x, axis=axis)

def _gelu(x):
    return jax.nn.gelu(x, approximate=True)

def _silu(x):
    return jax.nn.silu(x)

def _sigmoid(x):
    return jax.nn.sigmoid(x)

def _layernorm(x, axis=-1, eps=1e-05):
    m = jnp.mean(x, axis=axis, keepdims=True)
    v = jnp.var(x, axis=axis, keepdims=True)
    return (x - m) / jnp.sqrt(v + eps)

def _scatter_add(tgt, idx, src, axis=0):
    return tgt.at[idx].add(src)

def _segment_sum(src, seg, n):
    return jax.ops.segment_sum(src, seg, n)
kernel_name = 'mk_metaformer_d1_conv_nchw128_r2_2fcd9e'

def setup_inputs(seed: int=0):
    np.random.seed(seed)
    _w = jnp.asarray

    def _rec_inputs():
        import jax
        import jax.numpy as jnp
        _gk = jax.random.key(seed)
        x = -0.0005207 + 1.001 * jax.random.normal(jax.random.fold_in(_gk, 1), (4, 64, 32, 32), jnp.float32)
        return x
    x = _rec_inputs()

    def _L0_conv_setup():
        import jax, jax.numpy as jnp
        import numpy as np
        BN_EPS = 1e-05

        def conv2d(x, w, b, s, p):
            out = jax.lax.conv_general_dilated(x, w, (s, s), [(p, p), (p, p)], dimension_numbers=('NCHW', 'OIHW', 'NCHW'))
            return out + b[None, :, None, None]

        def deform_conv2d(x, offset, mask, weight, s, p):
            B, C, H, W = x.shape
            O, _, k, _ = weight.shape
            T = k * k
            Ho, Wo = (offset.shape[2], offset.shape[3])
            off = offset.reshape(B, T, 2, Ho, Wo)
            ii = jnp.repeat(jnp.arange(k), k).astype(x.dtype)
            jj = jnp.tile(jnp.arange(k), k).astype(x.dtype)
            base_y = (jnp.arange(Ho) * s - p).astype(x.dtype)
            base_x = (jnp.arange(Wo) * s - p).astype(x.dtype)
            py = base_y[None, None, :, None] + ii[None, :, None, None] + off[:, :, 0]
            px = base_x[None, None, None, :] + jj[None, :, None, None] + off[:, :, 1]
            y0 = jnp.floor(py)
            x0 = jnp.floor(px)
            ly = py - y0
            lx = px - x0
            y0i = y0.astype(jnp.int32)
            x0i = x0.astype(jnp.int32)
            x_flat = x.reshape(B, C, H * W)

            def gather(yy, xx):
                valid = ((yy >= 0) & (yy < H) & (xx >= 0) & (xx < W)).astype(x.dtype)
                idx = jnp.clip(yy, 0, H - 1) * W + jnp.clip(xx, 0, W - 1)
                idx_f = jnp.broadcast_to(idx.reshape(B, 1, -1), (B, C, T * Ho * Wo))
                g = jnp.take_along_axis(x_flat, idx_f, axis=2).reshape(B, C, T, Ho, Wo)
                return g * valid[:, None]
            val = ((1 - ly) * (1 - lx))[:, None] * gather(y0i, x0i) + ((1 - ly) * lx)[:, None] * gather(y0i, x0i + 1) + (ly * (1 - lx))[:, None] * gather(y0i + 1, x0i) + (ly * lx)[:, None] * gather(y0i + 1, x0i + 1)
            val = val * mask[:, None]
            w_flat = weight.reshape(O, C, T)
            return jnp.einsum('bcthw,oct->bohw', val, w_flat)
        key = jax.random.key(seed)
        ks = jax.random.split(key, 8)
        B, C1, C2, H, W, k = (4, 64, 64, 32, 32, 3)
        fan_in = C1 * k * k
        return {'x': jax.random.normal(ks[0], (B, C1, H, W), jnp.float32), 'offset_w': 0.01 * jax.random.normal(ks[1], (2 * k * k, C1, k, k), jnp.float32), 'offset_b': jnp.zeros((2 * k * k,), jnp.float32), 'mask_w': 0.01 * jax.random.normal(ks[2], (k * k, C1, k, k), jnp.float32), 'mask_b': jnp.zeros((k * k,), jnp.float32), 'weight': jax.random.normal(ks[3], (C2, C1, k, k), jnp.float32) / np.sqrt(fan_in), 'bn_gamma': 0.5 + jax.random.uniform(ks[4], (C2,), jnp.float32), 'bn_beta': 0.1 * jax.random.normal(ks[5], (C2,), jnp.float32), 'bn_mean': 0.1 * jax.random.normal(ks[6], (C2,), jnp.float32), 'bn_var': 0.5 + jax.random.uniform(ks[7], (C2,), jnp.float32)}
    _L0_conv_all = _L0_conv_setup()
    _L0_conv_in = {k: v for k, v in _L0_conv_all.items() if k in ('offset_w', 'offset_b', 'mask_w', 'mask_b', 'weight', 'bn_gamma', 'bn_beta', 'bn_mean', 'bn_var')}
    del _L0_conv_all

    def _L0_ffn_setup():
        import jax, jax.numpy as jnp
        import numpy as np
        PADDED_SL = 4096
        TEMPERATURE = 1.0
        SIGMA_POW = 0.25

        def _stu_conv(phi, u, n):
            b, sl, d = u.shape
            sgn = jnp.where(jnp.arange(sl) % 2 == 0, 1.0, -1.0).astype(u.dtype)
            sgn3 = sgn[None, :, None]
            Vf = jnp.fft.rfft(phi, n=n, axis=0)
            Uf_p = jnp.fft.rfft(u, n=n, axis=1)
            Uf_m = jnp.fft.rfft(u * sgn3, n=n, axis=1)
            U_plus = jnp.fft.irfft(Vf[None, :, :, None] * Uf_p[:, :, None, :], n=n, axis=1)[:, :sl]
            U_minus = jnp.fft.irfft(Vf[None, :, :, None] * Uf_m[:, :, None, :], n=n, axis=1)[:, :sl]
            U_minus = U_minus * sgn[None, :, None, None]
            return (U_plus, U_minus)

        def _compute_spectral(u, sigma, phi, Mpp, Mpm):
            U_plus, U_minus = _stu_conv(phi, u, PADDED_SL)
            s = sigma ** SIGMA_POW
            out = jnp.einsum('btkd,k,kde->bte', U_plus, s, Mpp)
            out = out + jnp.einsum('btkd,k,kde->bte', U_minus, s, Mpm)
            return out

        def _compute_ar_u(Mu, u):
            sl = u.shape[1]
            out = jnp.zeros(u.shape[:2] + (Mu.shape[-1],), dtype=u.dtype)
            for i in range(Mu.shape[0]):
                ui = jnp.pad(u, ((0, 0), (i, 0), (0, 0)))[:, :sl]
                out = out + jnp.einsum('btd,de->bte', ui, Mu[i])
            return out

        def _stu(u, sigma, phi, Mu, Mpp, Mpm):
            return _compute_spectral(u, sigma, phi, Mpp, Mpm) + _compute_ar_u(Mu, u)
        key = jax.random.key(seed)
        ks = jax.random.split(key, 8)
        b, sl, d, K, k_u = (2, 2048, 64, 16, 3)
        x = jax.random.normal(ks[0], (b, sl, d), dtype=jnp.float32)
        sigma = jax.random.uniform(ks[1], (K,), dtype=jnp.float32, minval=0.001, maxval=1.0)
        phi = jax.random.normal(ks[2], (sl, K), dtype=jnp.float32) / np.sqrt(sl)
        M_u = jax.random.normal(ks[3], (4, k_u, d, d), dtype=jnp.float32) * 0.02
        M_phi_plus = jax.random.normal(ks[4], (4, K, d, d), dtype=jnp.float32) * 0.02
        M_phi_minus = jax.random.normal(ks[5], (4, K, d, d), dtype=jnp.float32) * 0.02
        log_weights = jnp.ones((4,), dtype=jnp.float32)
        u01 = jax.random.uniform(ks[6], (4,), dtype=jnp.float32, minval=1e-06, maxval=1.0 - 1e-06)
        gumbel = -jnp.log(-jnp.log(u01))
        return {'x': x, 'sigma': sigma, 'phi': phi, 'M_u': M_u, 'M_phi_plus': M_phi_plus, 'M_phi_minus': M_phi_minus, 'log_weights': log_weights, 'gumbel': gumbel}
    _L0_ffn_all = _L0_ffn_setup()
    _L0_ffn_in = {k: v for k, v in _L0_ffn_all.items() if k in ('sigma', 'phi', 'M_u', 'M_phi_plus', 'M_phi_minus', 'log_weights', 'gumbel')}
    del _L0_ffn_all
    return {'x': x, 'L0_conv_offset_w': _L0_conv_in['offset_w'], 'L0_conv_offset_b': _L0_conv_in['offset_b'], 'L0_conv_mask_w': _L0_conv_in['mask_w'], 'L0_conv_mask_b': _L0_conv_in['mask_b'], 'L0_conv_weight': _L0_conv_in['weight'], 'L0_conv_bn_gamma': _L0_conv_in['bn_gamma'], 'L0_conv_bn_beta': _L0_conv_in['bn_beta'], 'L0_conv_bn_mean': _L0_conv_in['bn_mean'], 'L0_conv_bn_var': _L0_conv_in['bn_var'], 'L0_ffn_sigma': _L0_ffn_in['sigma'], 'L0_ffn_phi': _L0_ffn_in['phi'], 'L0_ffn_M_u': _L0_ffn_in['M_u'], 'L0_ffn_M_phi_plus': _L0_ffn_in['M_phi_plus'], 'L0_ffn_M_phi_minus': _L0_ffn_in['M_phi_minus'], 'L0_ffn_log_weights': _L0_ffn_in['log_weights'], 'L0_ffn_gumbel': _L0_ffn_in['gumbel']}

def reference(x, L0_conv_offset_w, L0_conv_offset_b, L0_conv_mask_w, L0_conv_mask_b, L0_conv_weight, L0_conv_bn_gamma, L0_conv_bn_beta, L0_conv_bn_mean, L0_conv_bn_var, L0_ffn_sigma, L0_ffn_phi, L0_ffn_M_u, L0_ffn_M_phi_plus, L0_ffn_M_phi_minus, L0_ffn_log_weights, L0_ffn_gumbel):
    import jax
    import jax.numpy as jnp

    def _L0_conv_ref(x, offset_w, offset_b, mask_w, mask_b, weight, bn_gamma, bn_beta, bn_mean, bn_var):
        import jax, jax.numpy as jnp
        import numpy as np
        BN_EPS = 1e-05

        def conv2d(x, w, b, s, p):
            out = jax.lax.conv_general_dilated(x, w, (s, s), [(p, p), (p, p)], dimension_numbers=('NCHW', 'OIHW', 'NCHW'))
            return out + b[None, :, None, None]

        def deform_conv2d(x, offset, mask, weight, s, p):
            B, C, H, W = x.shape
            O, _, k, _ = weight.shape
            T = k * k
            Ho, Wo = (offset.shape[2], offset.shape[3])
            off = offset.reshape(B, T, 2, Ho, Wo)
            ii = jnp.repeat(jnp.arange(k), k).astype(x.dtype)
            jj = jnp.tile(jnp.arange(k), k).astype(x.dtype)
            base_y = (jnp.arange(Ho) * s - p).astype(x.dtype)
            base_x = (jnp.arange(Wo) * s - p).astype(x.dtype)
            py = base_y[None, None, :, None] + ii[None, :, None, None] + off[:, :, 0]
            px = base_x[None, None, None, :] + jj[None, :, None, None] + off[:, :, 1]
            y0 = jnp.floor(py)
            x0 = jnp.floor(px)
            ly = py - y0
            lx = px - x0
            y0i = y0.astype(jnp.int32)
            x0i = x0.astype(jnp.int32)
            x_flat = x.reshape(B, C, H * W)

            def gather(yy, xx):
                valid = ((yy >= 0) & (yy < H) & (xx >= 0) & (xx < W)).astype(x.dtype)
                idx = jnp.clip(yy, 0, H - 1) * W + jnp.clip(xx, 0, W - 1)
                idx_f = jnp.broadcast_to(idx.reshape(B, 1, -1), (B, C, T * Ho * Wo))
                g = jnp.take_along_axis(x_flat, idx_f, axis=2).reshape(B, C, T, Ho, Wo)
                return g * valid[:, None]
            val = ((1 - ly) * (1 - lx))[:, None] * gather(y0i, x0i) + ((1 - ly) * lx)[:, None] * gather(y0i, x0i + 1) + (ly * (1 - lx))[:, None] * gather(y0i + 1, x0i) + (ly * lx)[:, None] * gather(y0i + 1, x0i + 1)
            val = val * mask[:, None]
            w_flat = weight.reshape(O, C, T)
            return jnp.einsum('bcthw,oct->bohw', val, w_flat)
        s, p = (1, 1)
        offset = conv2d(x, offset_w, offset_b, s, p)
        mask = jax.nn.sigmoid(conv2d(x, mask_w, mask_b, s, p))
        out = deform_conv2d(x, offset, mask, weight, s, p)
        scale = bn_gamma / jnp.sqrt(bn_var + BN_EPS)
        out = (out - bn_mean[None, :, None, None]) * scale[None, :, None, None] + bn_beta[None, :, None, None]
        return out * jax.nn.sigmoid(out)

    def _L0_ffn_ref(x, sigma, phi, M_u, M_phi_plus, M_phi_minus, log_weights, gumbel):
        import jax, jax.numpy as jnp
        import numpy as np
        PADDED_SL = 4096
        TEMPERATURE = 1.0
        SIGMA_POW = 0.25

        def _stu_conv(phi, u, n):
            b, sl, d = u.shape
            sgn = jnp.where(jnp.arange(sl) % 2 == 0, 1.0, -1.0).astype(u.dtype)
            sgn3 = sgn[None, :, None]
            Vf = jnp.fft.rfft(phi, n=n, axis=0)
            Uf_p = jnp.fft.rfft(u, n=n, axis=1)
            Uf_m = jnp.fft.rfft(u * sgn3, n=n, axis=1)
            U_plus = jnp.fft.irfft(Vf[None, :, :, None] * Uf_p[:, :, None, :], n=n, axis=1)[:, :sl]
            U_minus = jnp.fft.irfft(Vf[None, :, :, None] * Uf_m[:, :, None, :], n=n, axis=1)[:, :sl]
            U_minus = U_minus * sgn[None, :, None, None]
            return (U_plus, U_minus)

        def _compute_spectral(u, sigma, phi, Mpp, Mpm):
            U_plus, U_minus = _stu_conv(phi, u, PADDED_SL)
            s = sigma ** SIGMA_POW
            out = jnp.einsum('btkd,k,kde->bte', U_plus, s, Mpp)
            out = out + jnp.einsum('btkd,k,kde->bte', U_minus, s, Mpm)
            return out

        def _compute_ar_u(Mu, u):
            sl = u.shape[1]
            out = jnp.zeros(u.shape[:2] + (Mu.shape[-1],), dtype=u.dtype)
            for i in range(Mu.shape[0]):
                ui = jnp.pad(u, ((0, 0), (i, 0), (0, 0)))[:, :sl]
                out = out + jnp.einsum('btd,de->bte', ui, Mu[i])
            return out

        def _stu(u, sigma, phi, Mu, Mpp, Mpm):
            return _compute_spectral(u, sigma, phi, Mpp, Mpm) + _compute_ar_u(Mu, u)
        T = x.shape[1]
        outs = []
        for i, frac in enumerate((1, 2, 4, 8)):
            xi = x[:, :T // frac]
            si = _stu(xi, sigma, phi, M_u[i], M_phi_plus[i], M_phi_minus[i])
            si = jnp.pad(si, ((0, 0), (0, T - si.shape[1]), (0, 0)))
            outs.append(si)
        y_soft = jax.nn.softmax((log_weights + gumbel) / TEMPERATURE)
        y_hard = jax.nn.one_hot(jnp.argmax(y_soft), 4, dtype=y_soft.dtype)
        weights = y_hard - jax.lax.stop_gradient(y_soft) + y_soft
        stacked = jnp.stack(outs, axis=-1)
        return jnp.sum(stacked * weights, axis=-1)

    def _gn(v, G=32, eps=1e-05):
        B_, C_, H_, W_ = v.shape
        g = v.reshape(B_, G, C_ // G, H_, W_)
        m = jnp.mean(g, axis=(2, 3, 4), keepdims=True)
        s = jnp.var(g, axis=(2, 3, 4), keepdims=True)
        return ((g - m) / jnp.sqrt(s + eps)).reshape(v.shape)

    def _ln_c(v, eps=1e-06):
        m = jnp.mean(v, axis=1, keepdims=True)
        s = jnp.var(v, axis=1, keepdims=True)
        return (v - m) / jnp.sqrt(s + eps)

    def _ln_t(v, eps=1e-05):
        m = jnp.mean(v, axis=-1, keepdims=True)
        s = jnp.var(v, axis=-1, keepdims=True)
        return (v - m) / jnp.sqrt(s + eps)

    def _to_tokens(v):
        B_, C_, H_, W_ = v.shape
        return v.reshape(B_, C_, H_ * W_).transpose(0, 2, 1)

    def _from_tokens(t, like):
        B_, C_, H_, W_ = like.shape
        return t.transpose(0, 2, 1).reshape(B_, C_, H_, W_)
    x = x + _L0_conv_ref(_ln_c(x), L0_conv_offset_w, L0_conv_offset_b, L0_conv_mask_w, L0_conv_mask_b, L0_conv_weight, L0_conv_bn_gamma, L0_conv_bn_beta, L0_conv_bn_mean, L0_conv_bn_var)
    t = _to_tokens(x)
    t = t + _L0_ffn_ref(_ln_t(t), L0_ffn_sigma, L0_ffn_phi, L0_ffn_M_u, L0_ffn_M_phi_plus, L0_ffn_M_phi_minus, L0_ffn_log_weights, L0_ffn_gumbel)
    x = _from_tokens(t, x)
    return x

_drawn_inputs = setup_inputs


def setup_inputs(seed=0):
    import zlib

    import numpy as np

    out = dict(_drawn_inputs(seed))
    spreads = {'L0_conv_offset_b': (0.0, 0.1), 'L0_ffn_log_weights': (1.0, 0.2)}
    factors = {}
    for name, (base, spread) in spreads.items():
        noise = np.random.default_rng([zlib.crc32(name.encode()), seed]).standard_normal(out[name].shape)
        drawn = base * np.exp(spread * noise) if base else spread * noise
        out[name] = jnp.asarray(drawn.astype(out[name].dtype))
    for name, factor in factors.items():
        out[name] = (out[name] * factor).astype(out[name].dtype)
    return out
```

```python
import numpy as np
import concourse.bass as bass
from concourse import mybir
from contextlib import ExitStack

F32, F16, I32 = mybir.dt.float32, mybir.dt.float16, mybir.dt.int32
ALU, ACT, AX = mybir.AluOpType, mybir.ActivationFunctionType, mybir.AxisListType

P = 128
B, C, H, W = 4, 64, 32, 32
T = H * W
BP = B // 2
NJ = T // (2 * P)
NQ = BP * NJ
BLK = 4
TAPS = 9
NOFF = 3 * TAPS
ROW = 4 * C
SIDE = H + 1
PH, PW = H + 2, W + 2
K = 16
HALF = T // 2
BRANCHES = 4
HLEN = HALF + 2
HPAD = P + 2
HROW = HPAD + HALF + 2
START = 1
LN1_EPS, LN2_EPS, BN_EPS = 1e-6, 1e-5, 1e-5
U_SCALE = 32.0
PHI_SCALE = 256.0
NSLOT = 4
SEGS = [(0, HALF // 8), (HALF // 8, HALF // 4), (HALF // 4, HALF // 2), (HALF // 2, HALF)]
UNITS = [(0, 0, 2, (2, 3)), (0, 2, 4, (4, 5)), (1, 0, 2, (6, 7)), (1, 2, 4, ())]
RSQRT_SEED = float(0x5F3759DF)


def metaformer_kernel(nc, x, offset_w, offset_b, mask_w, mask_b, weight, gamma, beta, mean, var,
                      sigma, phi, m_u, m_plus, m_minus, log_weights, gumbel, ident_in, grid_in, first_row_in, out):
    ctx = ExitStack()
    with ctx:
        def sb(name, shape, dt=F32):
            return ctx.enter_context(nc.sbuf_tensor(name, shape, dt))

        def sem(name):
            return ctx.enter_context(nc.semaphore(name))

        def dram(name, shape, dt=F32):
            return nc.dram_tensor(name, shape, dt, kind="Internal").ap()

        def ap(a, offset, dims):
            return bass.AP(a.tensor, offset, dims)

        padded = dram("padded", [B, PH, PW, C])
        table = dram("corner_table", [B * SIDE * SIDE, ROW])
        hankel = dram("filter_rows", [K, 4, HROW], F16)
        mix_d = dram("mix_matrices", [K, C, 4, 2, C])

        ident_swap = sb("ident_swap", [P, 2, P])
        ident, swap = ident_swap[:, 0, :], ident_swap[:, 1, :]
        grid = sb("grid", [P, 8, NOFF])
        first_row = sb("first_row", [P, NQ * BLK])
        zeros = sb("zeros", [P, PW * C // 16])
        ones = sb("ones", [32, P])
        off_bias = sb("off_bias", [P, NOFF])
        w_off_raw = sb("w_off_raw", [NOFF, C * TAPS])
        w_off_dup = sb("w_off_dup", [NOFF, TAPS, 2, C])
        w_off = sb("w_off", [P, TAPS, NOFF])
        w_raw = sb("w_raw", [C, C * TAPS])
        w_scaled = sb("w_scaled", [C, TAPS * C])
        w_main = sb("w_main", [P, 5, C])
        bn_col = sb("bn_col", [C, 2])
        bn_row = sb("bn_row", [1, 4, C])
        bias_row = sb("bias_row", [1, C])
        x_both = sb("x_both", [P, 2 * BP * T])
        x_ch = x_both[:, 0:BP * T].rearrange("c (b t) -> c b t", b=BP)
        x_rev = x_both[:, BP * T:2 * BP * T].rearrange("c (b t) -> c b t", b=BP)
        x_tok = sb("x_tok", [P, NQ, 2, 2, C])
        n_tok = sb("n_tok", [P, NQ, 2, 2, C])
        n_pad = sb("n_pad", [P, BP, 4, PH, W // 2])
        stat = sb("stat", [P, 6, 16])
        offs = sb("offs", [P, NQ, BLK, NOFF])
        mask = sb("mask", [P, NQ, BLK, TAPS])
        pos = sb("pos", [P, BLK, TAPS, 2])
        pos_i = sb("pos_i", [P, BLK, TAPS, 2], I32)
        corner = sb("corner", [P, BLK, TAPS, 2])
        frac = sb("frac", [P, BLK, TAPS, 2])
        anti = sb("anti", [P, BLK, TAPS, 2])
        my = sb("my", [P, 2, BLK, TAPS])
        idx_f = sb("idx_f", [P, BLK, TAPS])
        idx = sb("idx", [P, 2, BLK, TAPS], I32)
        wts = sb("wts", [P, 2, BLK, TAPS, 4])
        G = sb("G", [P, BLK, TAPS, ROW])
        V = sb("V", [P, BLK, TAPS * C])
        n_store = V[:].rearrange("s k f -> s (k f)")[:, 0:NQ * 4 * C].rearrange(
            "s (q b p c) -> s q b p c", q=NQ, b=2, p=2)
        vT = sb("vT", [P, 2, 5, P])
        expo = sb("expo", [P, 2, C])
        sil = sb("sil", [P, 2, C])
        cen = sb("cen", [P, 2, C])
        sq = sb("sq", [P, 2, C])
        st2 = sb("st2", [P, 6, 2])
        x2_tok = sb("x2_tok", [P, NQ, 2, 2, C])
        u_tok = sb("u_tok", [P, 2, 2, C])
        u_hi = sb("u_hi", [P, NQ, 2, 2 * C], F16)
        u_lo = sb("u_lo", [P, NQ, 2, 2 * C], F16)
        uT = sb("uT", [P, 2, BP, 1 + HALF])
        phi_sb = sb("phi_sb", [P, NJ, 2 * K])
        f_max = sb("f_max", [2 * K, 4])
        f_rows = sb("f_rows", [2 * K, 2, HROW], F16)
        f_diag = sb("f_diag", [2 * K, 2 * K])
        sig = sb("sig", [P, 6, 2 * K])
        br = sb("br", [P, 10, BRANCHES])
        mu_raw = sb("mu_raw", [P, BRANCHES, 3 * C])
        mu = sb("mu", [P, 4, 3, C])
        ring = sb("ring", [P, NSLOT * 2 * HLEN])
        ring_h = ring[:].bitcast(F16).rearrange("s (n p h c) -> s n p h c", n=NSLOT, p=2, h=2)
        ring_m = sb("ring_m", [P, NSLOT, 3, 2, C])
        u_conv = sb("u_conv", [P, 2, 512])
        o_sb = sb("o_sb", [P, 512])
        m_raw = ring[:, 0:BRANCHES * 2 * 8 * C].rearrange("d (r m k e) -> d r m k e", r=BRANCHES, m=2, k=8)
        m_acc = sb("m_acc", [P, 2, 8, C])
        m_out = x_both[:].rearrange("d (k s p e) -> d k s p e", k=8, s=4, p=2)

        bank = [ctx.enter_context(nc.psum_tensor(f"bank{i}", [P, 512], F32)) for i in range(8)]
        conv_ps, out_ps = bank[0:2], bank[2:4]
        val_ps, tail_ps = bank[4:6], bank[6]
        y_ps = tail_ps[:, 256:256 + 2 * C]

        s_x = [sem(f"s_x{i}") for i in range(BP)]
        s_ident, s_const, s_woff, s_w, s_bn, s_phi, s_mats, s_small = (
            sem(n) for n in ("s_ident", "s_const", "s_woff", "s_w", "s_bn", "s_phi", "s_mats", "s_small"))
        zeroed, border_stored, padded_stored = sem("zeroed"), sem("border_stored"), [sem(f"padded_stored{i}") for i in range(BP)]
        table_stored = [sem(f"table_stored{i}") for i in range(BP)]
        x_reversed = sem("x_reversed")
        x_turned, x_copied, n_ready, n_turned, n_copied = (
            sem(n) for n in ("x_turned", "x_copied", "n_ready", "n_turned", "n_copied"))
        woff_ready, woff_turned, woff_copied = sem("woff_ready"), sem("woff_turned"), sem("woff_copied")
        w_ready, w_turned, w_copied = sem("w_ready"), sem("w_turned"), sem("w_copied")
        phi_turned, f_rows_ready, f_rows_stored = sem("phi_turned"), sem("f_rows_ready"), sem("f_rows_stored")
        diag_ready, f_scale_ready = sem("diag_ready"), sem("f_scale_ready")
        mats_ready, mats_stored = sem("mats_ready"), sem("mats_stored")
        off_done, off_copied, mask_exp = sem("off_done"), sem("off_copied"), sem("mask_exp")
        br_ready, br_exp = sem("br_ready"), sem("br_exp")
        idx_ready = sem("idx_ready")
        gathered = [sem(f"gathered{i}") for i in range(BLK)]
        v_ready = [sem(f"v_ready{i}") for i in range(BLK)]
        val_copied, y_done, y_exp, y_used, u_ready = (
            sem(n) for n in ("val_copied", "y_done", "y_exp", "y_used", "u_ready"))
        val_turned = [sem(f"val_turned{i}") for i in range(2)]
        u_turned, u_copied = sem("u_turned"), sem("u_copied")
        filt_loaded = [sem(f"filt_loaded{i}") for i in range(NSLOT)]
        filt_used = [sem(f"filt_used{i}") for i in range(NSLOT)]
        conv_done = [sem(f"conv_done{i}") for i in range(2)]
        conv_copied = [sem(f"conv_copied{i}") for i in range(2)]
        out_copied, out_stored = sem("out_copied"), sem("out_stored")
        dve_step = sem("dve_step")

        pool_marks, pe_marks, dve_marks = sem("pool_marks"), sem("pe_marks"), sem("dve_marks")

        N_SMALL = 4
        block = ctx.enter_context(nc.Block())

        @block.sync
        def _(sp):
            sp.dma_start(ident_swap[:], ident_in).then_inc(s_ident, 16)
            for bp in range(BP):
                sp.dma_start(x_ch[:, bp, :], ap(x, bp * 2 * C * T, [[T, P], [1, T]])).then_inc(s_x[bp], 16)
            sp.dma_start(w_off_raw[0:2 * TAPS, :], ap(offset_w, 0, [[C * TAPS, 2 * TAPS], [1, C * TAPS]])).then_inc(s_woff, 16)
            sp.dma_start(w_off_raw[2 * TAPS:NOFF, :], ap(mask_w, 0, [[C * TAPS, TAPS], [1, C * TAPS]])).then_inc(s_woff, 16)
            sp.dma_start(grid[:], grid_in).then_inc(s_const, 16)
            sp.dma_start(first_row[:], first_row_in).then_inc(s_const, 16)
            sp.dma_start(off_bias[:, 0:2 * TAPS], ap(offset_b, 0, [[0, P], [1, 2 * TAPS]])).then_inc(s_const, 16)
            sp.dma_start(off_bias[:, 2 * TAPS:NOFF], ap(mask_b, 0, [[0, P], [1, TAPS]])).then_inc(s_const, 16)
            sp.wait_ge(zeroed, 1)
            edge = PW * C
            for b in range(B):
                for r in (0, PH - 1):
                    sp.dma_start(ap(padded, (b * PH + r) * edge, [[edge // 16, 16], [1, edge // 16]]),
                                 zeros[0:16, :]).then_inc(border_stored, 16)
            for col in (0, PW - 1):
                sp.dma_start(ap(padded, edge + col * C, [[PH * edge, B], [edge, H], [1, C]]),
                             zeros[:, 0:C]).then_inc(border_stored, 16)
            sp.dma_start(w_raw[:], ap(weight, 0, [[C * TAPS, C], [1, C * TAPS]])).then_inc(s_w, 16)
            sp.dma_start(phi_sb[:], ap(phi, 0, [[2 * K, P], [2 * P * K, NJ], [1, 2 * K]])).then_inc(s_phi, 16)
            for i, v in enumerate((gamma, var)):
                sp.dma_start(bn_col[:, i:i + 1], ap(v, 0, [[1, C], [1, 1]])).then_inc(s_bn, 16)
            for i, v in enumerate((gamma, beta, mean, var)):
                sp.dma_start(bn_row[:, i, :], ap(v, 0, [[C, 1], [1, C]])).then_inc(s_bn, 16)
            sp.dma_start(sig[:, 0, 0:K], ap(sigma, 0, [[0, P], [1, K]])).then_inc(s_small, 16)
            sp.dma_start(sig[:, 0, K:2 * K], ap(sigma, 0, [[0, P], [1, K]])).then_inc(s_small, 16)
            sp.dma_start(br[:, 0, :], ap(log_weights, 0, [[0, P], [1, BRANCHES]])).then_inc(s_small, 16)
            sp.dma_start(br[:, 1, :], ap(gumbel, 0, [[0, P], [1, BRANCHES]])).then_inc(s_small, 16)
            sp.wait_ge(border_stored, 16 * (2 * B + 2))
            for bp in range(BP):
                sp.wait_ge(n_ready, bp + 1)
                for j in range(NJ):
                    for b2 in range(2):
                        b = 2 * bp + b2
                        dst = ap(padded, ((b * PH + 1 + H - 8 * (j + 1)) * PW + 1) * C, [[edge, 8], [2 * C, 16], [1, 2 * C]])
                        sp.dma_start(dst, n_store[:, 4 * bp + j, b2, :, :]).then_inc(padded_stored[bp], 16)
                sp.wait_ge(padded_stored[bp], 16 * 2 * NJ)
                for b in (2 * bp, 2 * bp + 1):
                    for cy in range(2):
                        sp.dma_start(ap(table, b * SIDE * SIDE * ROW + cy * 2 * C, [[SIDE * ROW, SIDE], [ROW, SIDE], [1, 2 * C]]),
                                     ap(padded, (b * PH + cy) * edge, [[edge, SIDE], [C, SIDE], [1, 2 * C]])
                                     ).then_inc(table_stored[bp], 16)
            for i, m in enumerate((m_plus, m_minus)):
                for kh in range(2):
                    for r in range(BRANCHES):
                        sp.dma_start(m_raw[C * kh:C * kh + C, r, i, :, :],
                                     ap(m, (r * K + 8 * kh) * C * C, [[C, C], [C * C, 8], [1, C]])).then_inc(s_mats, 16)
            for half in range(2):
                for r in range(BRANCHES):
                    sp.dma_start(mu_raw[C * half:C * half + C, r, :],
                                 ap(m_u, r * 3 * C * C, [[C, C], [C * C, 3], [1, C]])).then_inc(s_mats, 16)
            sp.wait_ge(f_rows_ready, 1)
            for par in range(2):
                sp.dma_start(ap(hankel, par * 2 * HROW, [[4 * HROW, K], [1, 2 * HROW]]),
                             f_rows[K * par:K * par + K].rearrange("k h c -> k (h c)")).then_inc(f_rows_stored, 16)
            sp.wait_ge(mats_ready, 1)
            for kh in range(2):
                sp.dma_start(ap(mix_d, 8 * kh * C * 8 * C, [[8 * C, C], [C * 8 * C, 8], [1, 8 * C]]),
                             m_out[C * kh:C * kh + C, :, :, :, :]).then_inc(mats_stored, 16)
            sp.wait_ge(f_rows_stored, 32)
            sp.wait_ge(mats_stored, 32)
            for n, (bp, t0, t1, _) in enumerate(UNITS):
                ncol = 2 + P * t1
                seg0, nseg = unit_ranges(t0, t1)
                with sp.Fori(0, 2) as i:
                    for kk in range(8):
                        s = kk % NSLOT
                        sp.wait_ge(filt_used[s], START + 4 * n + 2 * i + kk // NSLOT)
                        k = 8 * i + kk
                        sp.dma_start(ring_h[:, s].rearrange("s p h c -> s (p h) c")[:, :, 0:ncol],
                                     ap(hankel, k * 4 * HROW + HPAD - 2 - (P - 1), [[1, P], [HROW, 4], [1, ncol]])
                                     ).then_inc(filt_loaded[s], 16)
                        sp.dma_start(ring_m[:, s, 0:nseg, :, :],
                                     ap(mix_d, k * C * 8 * C + seg0 * 2 * C, [[0, 2], [8 * C, C], [1, nseg * 2 * C]])
                                     ).then_inc(filt_loaded[s], 16)

        @block.gpsimd
        def _(pool):
            for bp in range(BP):
                pool.wait_ge(table_stored[bp], 16 * 4)
                with pool.Fori(0, NJ // 2) as i:
                    for h in range(2):
                        q = 4 * bp + 2 * i + h
                        pool.wait_ge(idx_ready, q + 1)
                        for k in range(BLK):
                            pool.wait_ge(v_ready[k], START + q)
                            pool.sem_inc(pool_marks, 1)
                            for tap in range(TAPS):
                                pool.indirect_dma_start(
                                    G[:, k, tap, :], None, table,
                                    bass.IndirectOffsetOnAxis(ap=idx[:, h, k, tap:tap + 1], axis=0)
                                ).then_inc(gathered[k], 16)

        @block.vector
        def _(dve):
            steps = [0]

            def chain(ins):
                steps[0] += 1
                ins.then_inc(dve_step, 1)
                dve.wait_ge(dve_step, steps[0])

            def rsqrt(y, v, t):
                link(dve.tensor_scalar(t.bitcast(I32), v.bitcast(I32), 1, None, ALU.logical_shift_right))
                link(dve.tensor_scalar(y.bitcast(I32), t.bitcast(I32), -1.0, RSQRT_SEED, ALU.mult, ALU.add))
                for _ in range(3):
                    link(dve.scalar_tensor_tensor(t, y, -0.5, y, ALU.mult, ALU.mult))
                    link(dve.tensor_tensor(t, t, v, ALU.mult))
                    link(dve.scalar_tensor_tensor(y, t, 1.5, y, ALU.add, ALU.mult))

            link = chain

            for s in (*v_ready, y_used):
                dve.sem_inc(s, START)
            dve.memset(zeros[:], 0.0).then_inc(zeroed, 1)
            for bp in range(BP):
                dve.wait_ge(s_x[bp], 16)
                dve.tensor_copy(x_rev[:, bp, :], x_ch[:, bp, ::-1]).then_inc(x_reversed, 1)
            dve.memset(ones[:], 1.0)
            dve.memset(n_pad[:], 0.0)
            dve.memset(uT[:], 0.0)
            link(dve.memset(f_rows[:], 0.0))
            dve.wait_ge(s_woff, 32)
            raw = w_off_raw[:].rearrange("o (c t) -> o t c", t=TAPS)
            dve.tensor_copy(w_off_dup[:, :, 0, :], raw)
            dve.tensor_copy(w_off_dup[:, :, 1, :], raw).then_inc(woff_ready, 1)
            dve.wait_ge(s_const, 64)
            link(dve.tensor_tensor(grid[:], grid[:], off_bias[:].unsqueeze(1).broadcast_to([P, 8, NOFF]), ALU.subtract))
            for bp in range(BP):
                qs = slice(4 * bp, 4 * bp + 4)
                xs = x_tok[:, qs].rearrange("s q p b c -> s (q p b) c")
                ns = n_tok[:, qs].rearrange("s q p b c -> s (q p b) c")
                tmp = G[:, 2 * bp, 0:4, :].rearrange("s t r -> s (t r)").rearrange("s (g c) -> s g c", c=C)
                dve.wait_ge(x_copied, 2 * (bp + 1))
                link(dve.tensor_reduce(stat[:, 0, :], xs, AX.X, ALU.add))
                link(dve.tensor_scalar(stat[:, 1, :], stat[:, 0, :], 1.0 / C, None, ALU.mult))
                link(dve.tensor_tensor(ns, xs, stat[:, 1, :].unsqueeze(2).broadcast_to([P, 16, C]), ALU.subtract))
                link(dve.tensor_tensor(tmp, ns, ns, ALU.mult))
                link(dve.tensor_reduce(stat[:, 2, :], tmp, AX.X, ALU.add))
                link(dve.tensor_scalar(stat[:, 3, :], stat[:, 2, :], 1.0 / C, LN1_EPS, ALU.mult, ALU.add))
                rsqrt(stat[:, 4, :], stat[:, 3, :], stat[:, 5, :])
                link(dve.tensor_tensor(ns, ns, stat[:, 4, :].unsqueeze(2).broadcast_to([P, 16, C]), ALU.mult))
                for p in range(2):
                    last = dve.tensor_copy(n_store[:, qs, :, 1 - p, :], n_tok[:, qs, p])
                last.then_inc(n_ready, 1)

            def offsets(bp):
                for b2 in range(2):
                    dve.wait_ge(off_done, 2 * bp + b2 + 1)
                    dst = offs[:, 4 * bp:4 * bp + 4, 2 * b2:2 * b2 + 2, :].rearrange("s q k n -> s q (k n)")
                    last = dve.tensor_tensor(dst, grid[:].rearrange("s (q k) n -> s q (k n)", q=NJ),
                                             bank[4 + 2 * bp + b2][:, 0:8 * NOFF].rearrange("s (q n) -> s q n", q=NJ), ALU.subtract)
                last.then_inc(off_copied, 1)

            def masks(bp):
                m = mask[:, 4 * bp:4 * bp + 4].rearrange("s q k t -> s (q k t)")
                dve.wait_ge(mask_exp, bp + 1)
                link(dve.tensor_scalar(m, m, 1.0, None, ALU.add))
                link(dve.reciprocal(m, m))

            def positions(q, slot):
                o = offs[:, q] if isinstance(q, int) else offs[:, bass.ds(q, 1)].rearrange("s o k n -> s (o k) n")
                mk = mask[:, q] if isinstance(q, int) else mask[:, bass.ds(q, 1)].rearrange("s o k n -> s (o k) n")
                fr = first_row[:, bass.ds(q * BLK, BLK)]
                pk = pos[:].rearrange("s k t a -> s k (t a)")
                link(dve.tensor_scalar(pk, o[:, :, 0:2 * TAPS], 0.0, float(H + 1), ALU.max, ALU.min))
                link(dve.tensor_copy(pos_i[:], pos[:]))
                link(dve.tensor_tensor(corner[:], pos_i[:], pos[:], ALU.is_gt))
                link(dve.tensor_tensor(corner[:], pos_i[:], corner[:], ALU.subtract))
                link(dve.tensor_scalar(corner[:], corner[:], float(H), None, ALU.min))
                dve.tensor_tensor(frac[:], pos[:], corner[:], ALU.subtract)
                link(dve.scalar_tensor_tensor(idx_f[:], corner[:, :, :, 0], float(SIDE), corner[:, :, :, 1], ALU.mult, ALU.add))
                dve.tensor_tensor(idx[:, slot], idx_f[:], fr.unsqueeze(2).broadcast_to([P, BLK, TAPS]), ALU.add
                                  ).then_inc(idx_ready, 1)
                link(dve.tensor_scalar(anti[:], frac[:], -1.0, 1.0, ALU.mult, ALU.add))
                dve.tensor_tensor(my[:, 0], mk, anti[:, :, :, 0], ALU.mult)
                link(dve.tensor_tensor(my[:, 1], mk, frac[:, :, :, 0], ALU.mult))
                for cy in range(2):
                    dve.tensor_tensor(wts[:, slot, :, :, 2 * cy], my[:, cy], anti[:, :, :, 1], ALU.mult)
                    last = dve.tensor_tensor(wts[:, slot, :, :, 2 * cy + 1], my[:, cy], frac[:, :, :, 1], ALU.mult)
                link(last)

            offsets(0)
            masks(0)
            positions(0, 0)

            dve.wait_ge(s_w, 16)
            dve.wait_ge(s_bn, 16 * 6)
            bn = bn_row[:]
            link(dve.tensor_scalar(bn_col[:, 1:2], bn_col[:, 1:2], BN_EPS, None, ALU.add))
            rsqrt(st2[0:C, 0, 0:1], bn_col[:, 1:2], st2[0:C, 1, 0:1])
            link(dve.tensor_tensor(bn_col[:, 0:1], bn_col[:, 0:1], st2[0:C, 0, 0:1], ALU.mult))
            dve.tensor_scalar(w_scaled[:].rearrange("o (t c) -> o t c", t=TAPS),
                              w_raw[:].rearrange("o (c t) -> o t c", t=TAPS), bn_col[:, 0:1], None, ALU.mult
                              ).then_inc(w_ready, 1)
            link(dve.tensor_scalar(bn[:, 3, :], bn[:, 3, :], BN_EPS, None, ALU.add))
            rsqrt(expo[0:1, 0, :], bn[:, 3, :], expo[0:1, 1, :])
            link(dve.tensor_tensor(bn[:, 0, :], bn[:, 0, :], expo[0:1, 0, :], ALU.mult))
            link(dve.tensor_tensor(bn[:, 2, :], bn[:, 2, :], bn[:, 0, :], ALU.mult))
            link(dve.tensor_tensor(bias_row[:], bn[:, 1, :], bn[:, 2, :], ALU.subtract))
            phi_ps = bank[7][0:2 * K, :]
            dve.wait_ge(phi_turned, 1)
            link(dve.tensor_reduce(f_max[:, 0:1], phi_ps, AX.X, ALU.max, apply_absolute_value=True))
            link(dve.tensor_scalar(f_max[:, 0:1], f_max[:, 0:1], 1e-30, 1.0 / PHI_SCALE, ALU.max, ALU.mult))
            link(dve.reciprocal(f_max[:, 1:2], f_max[:, 0:1]))
            link(dve.tensor_scalar(f_rows[:, 0, HPAD:HPAD + HALF], phi_ps, f_max[:, 1:2], None, ALU.mult))
            dve.scalar_tensor_tensor(f_rows[:, 1, HPAD:HPAD + HALF], phi_ps, f_max[:, 1:2], f_rows[:, 0, HPAD:HPAD + HALF],
                                     ALU.mult, ALU.subtract).then_inc(f_rows_ready, 1)
            link(dve.reciprocal(f_max[:, 2:3], f_max[:, 1:2]))
            dve.tensor_scalar(f_diag[:], ident[0:2 * K, 0:2 * K], f_max[:, 2:3], None, ALU.mult).then_inc(diag_ready, 1)
            dve.wait_ge(s_small, 16 * N_SMALL)
            rsqrt(sig[:, 1, :], sig[:, 0, :], sig[:, 2, :])
            link(dve.tensor_tensor(sig[:, 1, :], sig[:, 1, :], sig[:, 0, :], ALU.mult))
            rsqrt(sig[:, 3, :], sig[:, 1, :], sig[:, 2, :])
            link(dve.tensor_tensor(sig[:, 3, :], sig[:, 3, :], sig[:, 1, :], ALU.mult))
            link(dve.tensor_tensor(br[:, 2, :], br[:, 0, :], br[:, 1, :], ALU.add))
            link(dve.tensor_reduce(br[:, 3, 0:1], br[:, 2, :], AX.X, ALU.max))
            dve.tensor_scalar(br[:, 4, :], br[:, 2, :], br[:, 3, 0:1], None, ALU.subtract).then_inc(br_ready, 1)
            for r in range(BRANCHES):
                dve.memset(br[:, 8, r:r + 1], float(BRANCHES - r))
            dve.wait_ge(br_exp, 1)
            link(dve.reciprocal(br[:, 3, 2:3], br[:, 3, 1:2]))
            link(dve.tensor_scalar(br[:, 6, :], br[:, 5, :], br[:, 3, 2:3], None, ALU.mult))
            link(dve.tensor_reduce(br[:, 3, 3:4], br[:, 6, :], AX.X, ALU.max))
            link(dve.scalar_tensor_tensor(br[:, 7, :], br[:, 6, :], br[:, 3, 3:4], br[:, 8, :], ALU.is_ge, ALU.mult))
            link(dve.tensor_reduce(br[:, 3, 0:1], br[:, 7, :], AX.X, ALU.max))
            link(dve.tensor_scalar(br[:, 7, :], br[:, 7, :], br[:, 3, 0:1], None, ALU.is_equal))
            link(dve.tensor_tensor(br[:, 7, :], br[:, 7, :], br[:, 6, :], ALU.subtract))
            link(dve.tensor_tensor(br[:, 9, :], br[:, 7, :], br[:, 6, :], ALU.add))
            dve.wait_ge(f_scale_ready, 1)
            link(dve.scalar_tensor_tensor(sig[:, 4, :], bank[0][:, 0:2 * K], 1.0 / U_SCALE, sig[:, 3, :], ALU.mult, ALU.mult))
            dve.wait_ge(s_mats, 16 * (4 * BRANCHES + 2 * BRANCHES))
            for r in range(BRANCHES):
                seg = 3 - r
                w = br[:, 9, r:r + 1]
                if r == 0:
                    dve.tensor_scalar(mu[:, seg].rearrange("d i e -> d (i e)"), mu_raw[:, r, :], w, None, ALU.mult)
                    link(dve.tensor_scalar(m_acc[:], m_raw[:, r], w, None, ALU.mult))
                else:
                    dve.scalar_tensor_tensor(mu[:, seg].rearrange("d i e -> d (i e)"), mu_raw[:, r, :], w,
                                             mu[:, seg + 1].rearrange("d i e -> d (i e)"), ALU.mult, ALU.add)
                    link(dve.scalar_tensor_tensor(m_acc[:].rearrange("d m k e -> d (m k e)"),
                                                  m_raw[:, r].rearrange("d m k e -> d (m k e)"), w,
                                                  m_acc[:].rearrange("d m k e -> d (m k e)"), ALU.mult, ALU.add))
                for par, op in enumerate((ALU.add, ALU.subtract)):
                    link(dve.tensor_tensor(m_out[:, :, seg, par, :], m_acc[:, 0], m_acc[:, 1], op))
                    for kh in range(2):
                        half = slice(C * kh, C * kh + C)
                        s = sig[half, 4, par * K + 8 * kh:par * K + 8 * kh + 8].unsqueeze(2).broadcast_to([C, 8, C])
                        last = dve.tensor_tensor(m_out[half, :, seg, par, :], m_out[half, :, seg, par, :], s, ALU.mult)
            last.then_inc(mats_ready, 1)
            offsets(1)
            masks(1)

            for bp in range(BP):
                dve.wait_ge(padded_stored[bp], 16 * 2 * NJ)


            def weigh(q, slot, k):
                dve.wait_ge(gathered[k], 16 * TAPS * (q + 1))
                if k % 2 == 0:
                    dve.wait_ge(val_turned[k // 2], START + q)
                g = G[:, k].rearrange("s t (n c) -> s (t n) c", c=C)
                w = wts[:, slot, k].rearrange("s t n -> s (t n)").unsqueeze(2).broadcast_to([P, 4 * TAPS, C])
                link(dve.tensor_tensor(g, g, w, ALU.mult))
                link(dve.tensor_tensor(G[:, k, :, 0:2 * C], G[:, k, :, 0:2 * C], G[:, k, :, 2 * C:4 * C], ALU.add))
                dve.tensor_tensor(V[:, k].rearrange("s (t c) -> s t c", c=C), G[:, k, :, 0:C], G[:, k, :, C:2 * C], ALU.add
                                  ).then_inc(v_ready[k], 1)

            def finish(q, b2):
                def at(t, *rest):
                    return t[(slice(None), bass.ds(q, 1)) + rest]
                xs = at(x_tok, slice(None), b2).rearrange("s o p c -> s (o p) c")
                x2 = at(x2_tok, slice(None), b2).rearrange("s o p c -> s (o p) c")
                hi = at(u_hi, slice(None), slice(C * b2, C * b2 + C)).rearrange("s o p c -> s (o p) c")
                lo = at(u_lo, slice(None), slice(C * b2, C * b2 + C)).rearrange("s o p c -> s (o p) c")
                u = u_tok[:, :, b2, :]
                dve.wait_ge(y_exp, 2 * q + b2 + 1)
                link(dve.tensor_scalar(expo[:], expo[:], 1.0, None, ALU.add))
                link(dve.reciprocal(sil[:], expo[:]))
                dve.tensor_tensor(sil[:], y_ps.rearrange("s (p c) -> s p c", p=2), sil[:], ALU.mult).then_inc(y_used, 1)
                dve.wait_ge(y_used, START + 2 * q + b2 + 1)
                link(dve.tensor_tensor(x2, xs, sil[:], ALU.add))
                dve.sem_inc(dve_marks, 1)
                link(dve.tensor_reduce(st2[:, 0, :], x2, AX.X, ALU.add))
                link(dve.tensor_scalar(st2[:, 1, :], st2[:, 0, :], 1.0 / C, None, ALU.mult))
                link(dve.tensor_tensor(cen[:], x2, st2[:, 1, :].unsqueeze(2).broadcast_to([P, 2, C]), ALU.subtract))
                link(dve.tensor_tensor(sq[:], cen[:], cen[:], ALU.mult))
                link(dve.tensor_reduce(st2[:, 2, :], sq[:], AX.X, ALU.add))
                link(dve.tensor_scalar(st2[:, 3, :], st2[:, 2, :], 1.0 / C, LN2_EPS, ALU.mult, ALU.add))
                rsqrt(st2[:, 4, :], st2[:, 3, :], st2[:, 5, :])
                if b2 == 0:
                    dve.wait_ge(u_turned, START + q)
                link(dve.tensor_tensor(u, cen[:], st2[:, 4, :].unsqueeze(2).broadcast_to([P, 2, C]), ALU.mult))
                link(dve.tensor_scalar(hi, u, U_SCALE, None, ALU.mult))
                dve.scalar_tensor_tensor(lo, u, U_SCALE, hi, ALU.mult, ALU.subtract).then_inc(u_ready, 1)

            def step(q, slot, last=False):
                if not last:
                    positions(q + 1, 1 - slot)
                weigh(q, slot, 0)
                weigh(q, slot, 1)
                weigh(q, slot, 2)
                finish(q, 0)
                weigh(q, slot, 3)
                finish(q, 1)

            per_loop = LINKS_PER_STEP * 2
            with dve.Fori(0, NQ // 2 - 1) as i:
                at0 = steps[0]

                def link(ins, i=i, at0=at0):
                    steps[0] += 1
                    ins.then_inc(dve_step, 1)
                    dve.wait_ge(dve_step, steps[0] + per_loop * i)
                step(2 * i, 0)
                step(2 * i + 1, 1)
                assert steps[0] - at0 == per_loop, (steps[0] - at0)
            steps[0] += per_loop * (NQ // 2 - 2)
            link = chain
            step(NQ - 2, 0)
            step(NQ - 1, 1, last=True)

        @block.scalar
        def _(act):
            for s in (u_copied, *conv_copied):
                act.sem_inc(s, START)
            for g in range(4):
                bp, jj = divmod(g, 2)
                act.wait_ge(x_turned, g + 1)
                act.copy(x_tok[:, 4 * bp + 2 * jj:4 * bp + 2 * jj + 2].rearrange("s q p b c -> s (q p b c)"),
                         bank[g][:]).then_inc(x_copied, 1)
            act.wait_ge(woff_turned, 1)
            act.copy(w_off[:], bank[6][:, 0:TAPS * NOFF].rearrange("c (t n) -> c t n", t=TAPS)).then_inc(woff_copied, 1)
            for g in range(4):
                bp, jj = divmod(g, 2)
                act.wait_ge(n_turned, g + 1)
                rows = slice(17 - 16 * jj, 33 - 16 * jj)
                for p in range(2):
                    src = bank[g][:, 256 * p:256 * p + 256].rearrange("c (y x) -> c y x", x=16)
                    act.copy(n_pad[:, bp, 2 - p, rows, :], src)
                    if p == 0:
                        last = act.copy(n_pad[:, bp, 0, rows, 1:16], src[:, :, 0:15])
                    else:
                        last = act.copy(n_pad[:, bp, 3, rows, 0:15], src[:, :, 1:16])
                last.then_inc(n_copied, 1)
            act.wait_ge(off_copied, 1)
            act.activation(mask[:, 0:4].rearrange("s q k t -> s (q k) t"), offs[:, 0:4].rearrange("s q k n -> s (q k) n")[:, :, 2 * TAPS:NOFF],
                           ACT.Exp).then_inc(mask_exp, 1)
            act.wait_ge(w_turned, 1)
            act.copy(w_main[:, 0:4, :], bank[3][:, 0:4 * C].rearrange("k (t o) -> k t o", t=4))
            act.copy(w_main[0:C, 4, :], bank[3][0:C, 4 * C:5 * C]).then_inc(w_copied, 1)
            act.wait_ge(br_ready, 1)
            act.activation(br[:, 5, :], br[:, 4, :], ACT.Exp, accum_out=br[:, 3, 1:2]).then_inc(br_exp, 1)
            act.wait_ge(off_copied, 2)
            act.activation(mask[:, 4:8].rearrange("s q k t -> s (q k) t"), offs[:, 4:8].rearrange("s q k n -> s (q k) n")[:, :, 2 * TAPS:NOFF],
                           ACT.Exp).then_inc(mask_exp, 1)

            def copy_values(q, b2):
                act.wait_ge(val_turned[b2], START + q + 1)
                for p in range(2):
                    act.copy(vT[:, p, 0:4, :], val_ps[p][:].rearrange("k (m s) -> k m s", m=4))
                act.copy(vT[0:C, :, 4, :], tail_ps[0:C, 0:256].rearrange("k (p s) -> k p s", p=2)).then_inc(val_copied, 1)

            def exp_y(q, b2):
                act.wait_ge(y_done, 2 * q + b2 + 1)
                act.wait_ge(y_used, START + 2 * q + b2)
                act.activation(expo[:], y_ps.rearrange("s (p c) -> s p c", p=2), ACT.Exp, scale=-1.0).then_inc(y_exp, 1)

            def copy_tokens(bp, q, j):
                act.wait_ge(u_turned, START + q + 1)
                act.copy(uT[:, :, bp, bass.ds(1 + P * j, P)],
                         val_ps[0][:, 0:256].rearrange("c (p s) -> c p s", p=2)).then_inc(u_copied, 1)

            with act.Fori(0, 2) as i:
                for b2 in range(2):
                    copy_values(i, b2)
                    exp_y(i, b2)
                copy_tokens(0, i, i)
            for n, (bp, t0, t1, side) in enumerate(UNITS):
                width = 2 * P * (t1 - t0)
                with act.Fori(0, 2) as i:
                    q = side[0] + i if side else None
                    actions = beside(bool(side), lambda b2: copy_values(q, b2), lambda b2: exp_y(q, b2),
                                     lambda: copy_tokens(side[0] // NJ, q, side[0] % NJ + i))
                    for m in range(16):
                        act.wait_ge(conv_done[m % 2], 16 * n + 8 * i + m // 2 + 1)
                        act.copy(u_conv[:, m % 2, 0:width], conv_ps[m % 2][:, 0:width]).then_inc(conv_copied[m % 2], 1)
                        for a in actions.get(m, ()):
                            a()
                act.wait_ge(filt_used[NSLOT - 1], START + 4 * (n + 1))
                if n:
                    act.wait_ge(out_stored, 16 * n)
                act.copy(o_sb[:, 0:width].rearrange("c (a p) -> c p a", p=2),
                         out_ps[n % 2][:, 0:width].rearrange("c (p a) -> c p a", p=2)).then_inc(out_copied, 1)
                act.wait_ge(out_copied, n + 1)
                act.dma_start(ap(out, bp * 2 * C * T + 2 * P * t0, [[T, P], [1, width]]), o_sb[:, 0:width]).then_inc(out_stored, 16)
            act.wait_ge(out_stored, 16 * len(UNITS))

        @block.tensor
        def _(pe):
            for s in (*val_turned, u_turned, *filt_used):
                pe.sem_inc(s, START)
            pe.wait_ge(s_ident, 16)
            for g in range(4):
                bp, jj = divmod(g, 2)
                if jj == 0:
                    pe.wait_ge(x_reversed, bp + 1)
                for j2 in range(2):
                    for p in range(2):
                        t = T - 255 - 256 * (2 * jj + j2) - p
                        last = pe.transpose(bank[g][:, P * (2 * j2 + p):P * (2 * j2 + p) + P], x_rev[:, bp, t:t + 255:2], ident)
                last.then_inc(x_turned, 1)
            pe.wait_ge(woff_ready, 1)
            for t in range(TAPS):
                last = pe.transpose(bank[6][:, NOFF * t:NOFF * t + NOFF], w_off_dup[:, t].rearrange("o h c -> o (h c)"),
                                    ident[0:NOFF, 0:NOFF])
            last.then_inc(woff_turned, 1)
            pe.wait_ge(s_phi, 16)
            for j in range(NJ):
                last = pe.transpose(bank[7][0:2 * K, P * j:P * j + P], phi_sb[:, j, :], ident)
            last.then_inc(phi_turned, 1)

            def turn_normalised(bp):
                pe.wait_ge(n_ready, bp + 1)
                pe.wait_ge(x_copied, 2 * (bp + 1))
                for jj in range(2):
                    for j2 in range(2):
                        for p in range(2):
                            last = pe.transpose(bank[2 * bp + jj][:, 256 * p + P * (1 - j2):256 * p + P * (1 - j2) + P],
                                                n_tok[:, 4 * bp + 2 * jj + j2, p].rearrange("s b c -> s (b c)"), ident)
                    last.then_inc(n_turned, 1)

            def convolve_offsets(bp):
                pe.wait_ge(n_copied, 2 * (bp + 1))
                for j in range(NJ):
                    for p in range(2):
                        for t in range(TAPS):
                            dy, dx = divmod(t, 3)
                            for b2 in range(2):
                                half = slice(C * b2, C * b2 + C)
                                col = (2 * j + p) * NOFF
                                last = pe.matmul(bank[4 + 2 * bp + b2][:, col:col + NOFF],
                                                 n_pad[half, bp, 3 - p - dx, 26 - 8 * j - dy:34 - 8 * j - dy, :].rearrange("c y x -> c (y x)"),
                                                 w_off[half, t, :], start=(t == 0), stop=(t == TAPS - 1))
                last.then_inc(off_done, 2)

            turn_normalised(0)
            pe.wait_ge(woff_copied, 1)
            convolve_offsets(0)
            turn_normalised(1)
            pe.wait_ge(w_ready, 1)
            pe.wait_ge(n_copied, 4)
            for m in range(5):
                rows = min(P, (TAPS - 2 * m) * C)
                last = pe.transpose(bank[3][0:rows, C * m:C * m + C], w_scaled[:, P * m:P * m + rows], ident[0:C, 0:C])
            last.then_inc(w_turned, 1)
            pe.wait_ge(diag_ready, 1)
            pe.matmul(bank[0][:, 0:2 * K], ones[:], f_diag[:], start=True, stop=True).then_inc(f_scale_ready, 1)
            convolve_offsets(1)

            def turn_values(q, b2):
                for k in (2 * b2, 2 * b2 + 1):
                    pe.wait_ge(v_ready[k], START + q + 1)
                pe.wait_ge(y_used, START + 2 * q + b2)
                if b2 == 0:
                    pe.wait_ge(u_copied, START + q)
                for p in range(2):
                    k = 2 * b2 + p
                    for m in range(4):
                        pe.transpose(val_ps[p][:, P * m:P * m + P], V[:, k, P * m:P * m + P], ident)
                    last = pe.transpose(tail_ps[0:C, P * p:P * p + P], V[:, k, 4 * P:4 * P + C], ident)
                last.then_inc(val_turned[b2], 1)

            def convolve_values(q, b2):
                pe.wait_ge(val_copied, 2 * q + b2 + 1)
                for p in range(2):
                    y = y_ps[:, C * p:C * p + C]
                    pe.matmul(y, ones[0:1, :], bias_row[:], start=True, stop=False)
                    for m in range(5):
                        rows = min(P, (TAPS - 2 * m) * C)
                        last = pe.matmul(y, vT[0:rows, p, m, :], w_main[0:rows, m, :], start=False, stop=(m == 4))
                last.then_inc(y_done, 1)

            def turn_tokens(q):
                pe.wait_ge(u_ready, 2 * q + 2)
                for p in range(2):
                    last = pe.matmul(val_ps[0][:, P * p:P * p + P], u_tok[:, p].rearrange("s b c -> s (b c)"), swap,
                                     start=True, stop=True)
                last.then_inc(u_turned, 1)

            pe.wait_ge(w_copied, 1)
            with pe.Fori(0, 2) as i:
                for b2 in range(2):
                    turn_values(i, b2)
                    convolve_values(i, b2)
                turn_tokens(i)

            for n, (bp, t0, t1, side) in enumerate(UNITS):
                blocks = t1 - t0
                width = P * blocks
                acc = out_ps[n % 2]
                seg0, nseg = unit_ranges(t0, t1)

                def ranges():
                    for s in range(seg0, seg0 + nseg):
                        yield s, max(SEGS[s][0], P * t0), min(SEGS[s][1], P * t1)

                def convolve(m, i):
                    kk, par = divmod(m, 2)
                    slot = kk % NSLOT
                    if par == 0:
                        pe.wait_ge(filt_loaded[slot], 32 * (4 * n + 2 * i + kk // NSLOT + 1))
                    pe.wait_ge(conv_copied[m % 2], START + 16 * n + 8 * i + m // 2)
                    for p in range(2):
                        src, shift = (p, 0) if par == 0 else (1 - p, 1 - p)
                        for j in range(t1):
                            o = max(t0, j)
                            cols = P * (t1 - o)
                            dst = conv_ps[m % 2][:, p * width + P * (o - t0):p * width + P * (o - t0) + cols]
                            c0 = 2 + P * (o - j) - shift
                            parts = ((u_hi, 0), (u_hi, 1), (u_lo, 0))
                            for e, (u, part) in enumerate(parts):
                                last = pe.matmul(dst, u[:, 4 * bp + j, src, :], ring_h[:, slot, par, part, c0:c0 + cols],
                                                 start=(j == 0 and e == 0), stop=(j == t1 - 1 and e == 2))
                    last.then_inc(conv_done[m % 2], 1)

                def mix(m, i):
                    kk, par = divmod(m, 2)
                    slot = kk % NSLOT
                    pe.wait_ge(conv_copied[m % 2], START + 16 * n + 8 * i + m // 2 + 1)
                    pe.sem_inc(pe_marks, 1)
                    uc = u_conv[:, m % 2, 0:2 * width].rearrange("c (p a) -> c p a", p=2)
                    o = acc[:, 0:2 * width].rearrange("c (p a) -> c p a", p=2)
                    for s, a0, a1 in ranges():
                        a0, a1 = a0 - P * t0, a1 - P * t0
                        for b2 in range(2):
                            half = slice(C * b2, C * b2 + C)
                            last = pe.matmul(o[half, :, a0:a1], ring_m[half, slot, s - seg0, par, :], uc[half, :, a0:a1],
                                             start=False, stop=False, skip_group_check=True)
                    if par == 1:
                        last.then_inc(filt_used[slot], 1)
                    return last

                if n >= 2:
                    pe.wait_ge(out_copied, n - 1)
                pe.wait_ge(u_copied, START + 4 * bp + t1)
                first = True
                for p in range(2):
                    for j in range(t0, t1):
                        pe.matmul(acc[:, p * width + P * (j - t0):p * width + P * (j - t0) + P],
                                  x2_tok[:, 4 * bp + j, p].rearrange("s b c -> s (b c)"), swap,
                                  start=first, stop=False, skip_group_check=True)
                        first = False
                for p in range(2):
                    for lag in range(3):
                        src, shift = (p - lag) % 2, (p - lag) // 2
                        for s, a0, a1 in ranges():
                            for b2 in range(2):
                                half = slice(C * b2, C * b2 + C)
                                pe.matmul(acc[half, p * width + a0 - P * t0:p * width + a1 - P * t0],
                                          mu[half, s, lag, :], uT[half, src, bp, 1 + a0 + shift:1 + a1 + shift],
                                          start=False, stop=False, skip_group_check=True)
                with pe.Fori(0, 2) as i:
                    q = side[0] + i if side else None
                    actions = beside(bool(side), lambda b2: turn_values(q, b2), lambda b2: convolve_values(q, b2),
                                     lambda: turn_tokens(q))
                    for m in range(16):
                        convolve(m, i)
                        if m:
                            mix(m - 1, i)
                        for a in actions.get(m, ()):
                            a()
                    mix(15, i)


LINKS_PER_STEP = 61


def unit_ranges(t0, t1):
    hit = [s for s, (a, b) in enumerate(SEGS) if a < P * t1 and b > P * t0]
    return hit[0], len(hit)


def beside(side, values, convolved, tokens):
    if not side:
        return {}
    return {1: [lambda: values(0)], 3: [lambda: convolved(0)], 5: [lambda: values(1)],
            7: [lambda: convolved(1)], 12: [tokens]}


_INS = ['x', 'L0_conv_offset_w', 'L0_conv_offset_b', 'L0_conv_mask_w', 'L0_conv_mask_b', 'L0_conv_weight',
        'L0_conv_bn_gamma', 'L0_conv_bn_beta', 'L0_conv_bn_mean', 'L0_conv_bn_var', 'L0_ffn_sigma', 'L0_ffn_phi',
        'L0_ffn_M_u', 'L0_ffn_M_phi_plus', 'L0_ffn_M_phi_minus', 'L0_ffn_log_weights', 'L0_ffn_gumbel']


def constants():
    s = P - 1 - np.arange(P)
    grid = np.zeros((P, 2 * NJ, NOFF), np.float32)
    for j in range(NJ):
        for p in range(2):
            for t in range(TAPS):
                grid[:, 2 * j + p, 2 * t] = H + 1 - (8 * j + s // 16 + t // 3)
                grid[:, 2 * j + p, 2 * t + 1] = W + 1 - (2 * (s % 16) + p + t % 3)
    first = np.array([(2 * (q // NJ) + k // 2) * SIDE * SIDE for q in range(NQ) for k in range(BLK)], np.float32)
    return {"ident": np.stack([np.eye(P), np.eye(P)[::-1]], 1).astype(np.float32), "grid": grid, "first_row": np.tile(first, (P, 1))}


def kernel(**inputs):
    import numpy as _np
    import concourse.bacc as _bacc
    from concourse import mybir as _mybir
    from concourse.bass_utils import run_bass_kernel_spmd as _run

    nc = _bacc.Bacc("TRN2", target_bir_lowering=False, num_devices=1)
    arrays, args = {}, []
    for name, a in [(n, inputs[n]) for n in _INS] + list(constants().items()):
        a = _np.ascontiguousarray(a)
        arrays[f"in_{name}_dram"] = a
        args.append(nc.dram_tensor(f"in_{name}_dram", a.shape, _mybir.dt.from_np(a.dtype), kind="ExternalInput").ap())
    args.append(nc.dram_tensor("out_0_dram", (B, C, H, W), _mybir.dt.float32, kind="ExternalOutput").ap())
    metaformer_kernel(nc, *args)
    r = _run(nc, [arrays], core_ids=[0])
    return r.results[0]["out_0_dram"]
```

```python
import numpy as np
import concourse.bass as bass
from concourse import mybir
from contextlib import ExitStack

F32, F16, I32 = mybir.dt.float32, mybir.dt.float16, mybir.dt.int32
ALU, ACT, AX = mybir.AluOpType, mybir.ActivationFunctionType, mybir.AxisListType

P = 128
B, C, H, W = 4, 64, 32, 32
T = H * W
BP = B // 2
NJ = T // (2 * P)
NQ = BP * NJ
NR = 2 * NQ
BLK = 4
TAPS = 9
NOFF = 3 * TAPS
NCH = 32
ROW = 4 * C
SIDE = H + 1
PH, PW = H + 2, W + 2
K = 16
HALF = T // 2
BRANCHES = 4
HLEN = HALF + 2
HPAD = P + 2
HROW = HPAD + HALF + 2
START = 2
LN1_EPS, LN2_EPS, BN_EPS = 1e-6, 1e-5, 1e-5
U_SCALE = 32.0
PHI_SCALE = 256.0
NSLOT = 4
SEGS = [(0, HALF // 8), (HALF // 8, HALF // 4), (HALF // 4, HALF // 2), (HALF // 2, HALF)]
RSQRT_SEED = float(0x5F3759DF)
TAP_HALVES = (range(0, 5), range(5, 9))
NCOL = P + 1
WARM_UP, WARM_UP_UNITS = 9, 5
PASSES = [(n, tuple(range(n % NJ + 1))) for n in range(NQ)]


def metaformer_kernel(nc, x, offset_w, offset_b, mask_w, mask_b, weight, gamma, beta, mean, var,
                      sigma, phi, m_u, m_plus, m_minus, log_weights, gumbel, ident_in, grid_in, first_row_in, out):
    ctx = ExitStack()
    with ctx:
        def sb(name, shape, dt=F32):
            return ctx.enter_context(nc.sbuf_tensor(name, shape, dt))

        def sem(name):
            return ctx.enter_context(nc.semaphore(name))

        def dram(name, shape, dt=F32):
            return nc.dram_tensor(name, shape, dt, kind="Internal").ap()

        def ap(a, offset, dims):
            return bass.AP(a.tensor, offset, dims)

        padded = dram("padded", [B, PH, PW, C])
        table = [dram(f"corner_table{i}", [2 * SIDE * SIDE, ROW]) for i in range(BP)]
        hankel = dram("filter_rows", [K, 4, HROW], F16)
        mix_d = dram("mix_matrices", [K, C, 4, 3, C])

        ident_swap = sb("ident_swap", [P, 3, P])
        ident, swap = ident_swap[:, 0, :], ident_swap[:, 1, :]
        fold = ident_swap[:, 2, 0:C]
        grid = sb("grid", [P, 8, NOFF])
        first_row = sb("first_row", [P, BLK])
        zeros = sb("zeros", [P, PW * C // 16])
        ones = sb("ones", [K, P])
        off_bias = sb("off_bias", [P, NOFF])
        w_off_raw = sb("w_off_raw", [NOFF, C * TAPS])
        w_off_dup = sb("w_off_dup", [NOFF, TAPS, 2, C])
        w_off = sb("w_off", [P, TAPS, NCH])
        w_raw = sb("w_raw", [C, C * TAPS])
        w_scaled = sb("w_scaled", [C, TAPS * C])
        w_main = sb("w_main", [P, 5, C])
        bn_col = sb("bn_col", [C, 2])
        bn_row = sb("bn_row", [P, 4, C])
        x_both = sb("x_both", [P, 2 * BP * T])
        x_ch = x_both[:, 0:BP * T].rearrange("c (b t) -> c b t", b=BP)
        x_rev = x_both[:, BP * T:2 * BP * T].rearrange("c (b t) -> c b t", b=BP)
        x_tok = sb("x_tok", [P, NQ, 2, 2, C])
        n_tok = sb("n_tok", [P, NQ, 2, 2, C])
        n_pad = sb("n_pad", [P, BP, PH, PW])
        stat = sb("stat", [P, 6, 16])
        off_ch = sb("off_ch", [P, 2, 512])
        offs = sb("offs", [P, NQ, BLK, NOFF])
        mask = sb("mask", [P, NQ, BLK, TAPS])
        pos = sb("pos", [P, BLK, TAPS, 2])
        pos_i = sb("pos_i", [P, BLK, TAPS, 2], I32)
        corner = sb("corner", [P, BLK, TAPS, 2])
        frac = sb("frac", [P, BLK, TAPS, 2])
        anti = sb("anti", [P, BLK, TAPS, 2])
        my = sb("my", [P, 2, BLK, TAPS])
        idx_f = sb("idx_f", [P, BLK, TAPS])
        idx = sb("idx", [P, 2, BLK, TAPS], I32)
        wts = sb("wts", [P, 2, BLK, TAPS, 4])
        G = sb("G", [P, BLK, TAPS, ROW])
        V = sb("V", [P, 2, TAPS * C])
        n_store = sb("n_store", [P, NQ, 2, 2, C])
        vT = sb("vT", [P, 2, 5, P])
        expo = sb("expo", [P, 2, C])
        sil = sb("sil", [P, 2, C])
        cen = sb("cen", [P, 2, C])
        sq = sb("sq", [P, 2, C])
        st2 = sb("st2", [P, 6, 2])
        x2_tok = sb("x2_tok", [P, NR, 2, C])
        u_tok = sb("u_tok", [P, 2 * C])
        u_hi = sb("u_hi", [P, NQ, 2, 2, C], F16)
        u_lo = sb("u_lo", [P, NQ, 2, 2, C], F16)
        uT = sb("uT", [P, 2, BP, 1 + HALF])
        phi_sb = sb("phi_sb", [P, NJ, 2, K])
        f_max = sb("f_max", [K, 4])
        f_rows = sb("f_rows", [K, 2, 2, HROW], F16)
        f_diag = sb("f_diag", [K, K])
        sig = sb("sig", [P, 4, K])
        f_scale = sb("f_scale", [P, K])
        br = sb("br", [P, 10, BRANCHES])
        w_diag = sb("w_diag", [P, BRANCHES, 2, P])
        mu_raw = sb("mu_raw", [P, BRANCHES, 3 * C])
        mu = sb("mu", [P, 4, 3, C])
        ring = sb("ring", [P, NSLOT * 2 * HLEN])
        ring_h = ring[:].bitcast(F16).rearrange("s (n p h c) -> s n p h c", n=NSLOT, p=2, h=2)
        ring_m = sb("ring_m", [P, NSLOT, 2 * 3 * C])
        u_conv = sb("u_conv", [P, 2, 2, 2, P])
        o_sb = sb("o_sb", [P, 2, 2 * P])
        m_raw = ring[:, 0:BRANCHES * 2 * 8 * C].rearrange("d (r m k e) -> d r m k e", r=BRANCHES, m=2, k=8)
        m_out = x_both[:, 0:2 * 8 * 3 * C].rearrange("d (n k p e) -> d n k p e", n=2, k=8, p=3)

        bank = [ctx.enter_context(nc.psum_tensor(f"bank{i}", [P, 512], F32)) for i in range(8)]
        conv_ps, acc_ps = bank[0:2], bank[2:4]
        val_ps, tail_ps, off_ps = bank[4:6], bank[6], bank[7]
        y_ps = tail_ps[:, 256:256 + 2 * C]

        s_x = [sem(f"s_x{i}") for i in range(BP)]
        s_ident, s_const, s_woff, s_w, s_bn, s_phi, s_mats, s_small = (
            sem(n) for n in ("s_ident", "s_const", "s_woff", "s_w", "s_bn", "s_phi", "s_mats", "s_small"))
        zeroed, border_stored, padded_stored = sem("zeroed"), sem("border_stored"), [sem(f"padded_stored{i}") for i in range(BP)]
        table_stored = [sem(f"table_stored{i}") for i in range(BP)]
        x_reversed = sem("x_reversed")
        x_turned, x_copied, n_ready, n_turned, n_copied = (
            sem(n) for n in ("x_turned", "x_copied", "n_ready", "n_turned", "n_copied"))
        woff_ready, woff_turned, woff_copied = sem("woff_ready"), sem("woff_turned"), sem("woff_copied")
        w_ready, w_turned, w_copied = sem("w_ready"), sem("w_turned"), sem("w_copied")
        phi_turned, f_rows_ready, f_rows_stored = sem("phi_turned"), sem("f_rows_ready"), sem("f_rows_stored")
        diag_ready, f_scale_ready, f_scale_done = sem("diag_ready"), sem("f_scale_ready"), sem("f_scale_done")
        w_diag_ready, mats_summed = sem("w_diag_ready"), sem("mats_summed")
        mats_ready, mats_stored, mu_ready = sem("mats_ready"), [sem(f"mats_stored{i}") for i in range(2)], sem("mu_ready")
        off_done, off_laid, off_turned, off_copied, mask_exp = (
            sem(n) for n in ("off_done", "off_laid", "off_turned", "off_copied", "mask_exp"))
        br_ready, br_exp = sem("br_ready"), sem("br_exp")
        idx_ready = sem("idx_ready")
        gathered = [sem(f"gathered{i}") for i in range(BLK)]
        v_ready = [sem(f"v_ready{i}") for i in range(2)]
        val_copied, y_done, y_exp, y_used, u_ready = (
            sem(n) for n in ("val_copied", "y_done", "y_exp", "y_used", "u_ready"))
        val_turned = sem("val_turned")
        u_turned, u_copied = sem("u_turned"), sem("u_copied")
        filt_loaded = [sem(f"filt_loaded{i}") for i in range(NSLOT)]
        filt_used = [sem(f"filt_used{i}") for i in range(NSLOT)]
        conv_done = [sem(f"conv_done{i}") for i in range(2)]
        conv_copied = [sem(f"conv_copied{i}") for i in range(2)]
        out_copied, out_stored = sem("out_copied"), [sem(f"out_stored{i}") for i in range(2)]
        dve_step = sem("dve_step")

        pool_marks, pe_marks, dve_marks, act_marks = (sem(f"{n}_marks") for n in ("pool", "pe", "dve", "act"))

        N_SMALL = 3
        block = ctx.enter_context(nc.Block())

        @block.sync
        def _(sp):
            sp.dma_start(ident_swap[:], ident_in).then_inc(s_ident, 16)
            for bp in range(BP):
                sp.dma_start(x_ch[:, bp, :], ap(x, bp * 2 * C * T, [[T, P], [1, T]])).then_inc(s_x[bp], 16)
            sp.dma_start(w_off_raw[0:2 * TAPS, :], ap(offset_w, 0, [[C * TAPS, 2 * TAPS], [1, C * TAPS]])).then_inc(s_woff, 16)
            sp.dma_start(w_off_raw[2 * TAPS:NOFF, :], ap(mask_w, 0, [[C * TAPS, TAPS], [1, C * TAPS]])).then_inc(s_woff, 16)
            sp.dma_start(grid[:], grid_in).then_inc(s_const, 16)
            sp.dma_start(first_row[:], first_row_in).then_inc(s_const, 16)
            sp.dma_start(off_bias[:, 0:2 * TAPS], ap(offset_b, 0, [[0, P], [1, 2 * TAPS]])).then_inc(s_const, 16)
            sp.dma_start(off_bias[:, 2 * TAPS:NOFF], ap(mask_b, 0, [[0, P], [1, TAPS]])).then_inc(s_const, 16)
            sp.dma_start(sig[:, 0, :], ap(sigma, 0, [[0, P], [1, K]])).then_inc(s_small, 16)
            sp.dma_start(br[:, 0, :], ap(log_weights, 0, [[0, P], [1, BRANCHES]])).then_inc(s_small, 16)
            sp.dma_start(br[:, 1, :], ap(gumbel, 0, [[0, P], [1, BRANCHES]])).then_inc(s_small, 16)
            sp.wait_ge(zeroed, 1)
            edge = PW * C
            for b in range(B):
                for r in (0, PH - 1):
                    sp.dma_start(ap(padded, (b * PH + r) * edge, [[edge // 16, 16], [1, edge // 16]]),
                                 zeros[0:16, :]).then_inc(border_stored, 16)
            for col in (0, PW - 1):
                sp.dma_start(ap(padded, edge + col * C, [[PH * edge, B], [edge, H], [1, C]]),
                             zeros[:, 0:C]).then_inc(border_stored, 16)
            sp.dma_start(phi_sb[:], ap(phi, 0, [[2 * K, P], [2 * P * K, NJ], [1, 2 * K]])).then_inc(s_phi, 16)
            sp.wait_ge(border_stored, 16 * (2 * B + 2))
            def store_table(bp):
                sp.wait_ge(n_ready, bp + 1)
                for j in range(NJ):
                    for b2 in range(2):
                        b = 2 * bp + b2
                        dst = ap(padded, ((b * PH + 1 + H - 8 * (j + 1)) * PW + 1) * C, [[edge, 8], [2 * C, 16], [1, 2 * C]])
                        sp.dma_start(dst, n_store[:, 4 * bp + j, b2, :, :]).then_inc(padded_stored[bp], 16)
                sp.wait_ge(padded_stored[bp], 16 * 2 * NJ)
                for b2 in range(2):
                    for cy in range(2):
                        sp.dma_start(ap(table[bp], b2 * SIDE * SIDE * ROW + cy * 2 * C, [[SIDE * ROW, SIDE], [ROW, SIDE], [1, 2 * C]]),
                                     ap(padded, ((2 * bp + b2) * PH + cy) * edge, [[edge, SIDE], [C, SIDE], [1, 2 * C]])
                                     ).then_inc(table_stored[bp], 16)

            def load_matrices():
                for i, m in enumerate((m_plus, m_minus)):
                    for kh in range(2):
                        for r in range(BRANCHES):
                            sp.dma_start(m_raw[C * kh:C * kh + C, r, i, :, :],
                                          ap(m, (r * K + 8 * kh) * C * C, [[C, C], [C * C, 8], [1, C]])).then_inc(s_mats, 16)
                for half in range(2):
                    for r in range(BRANCHES):
                        sp.dma_start(mu_raw[C * half:C * half + C, r, :],
                                      ap(m_u, r * 3 * C * C, [[C, C], [C * C, 3], [1, C]])).then_inc(s_mats, 16)
            store_table(0)
            load_matrices()
            store_table(1)
            sp.wait_ge(f_rows_ready, 1)
            sp.dma_start(ap(hankel, 0, [[4 * HROW, K], [1, 4 * HROW]]), f_rows[:].rearrange("k p h c -> k (p h c)")
                         ).then_inc(f_rows_stored, 16)
            for r in range(BRANCHES):
                sp.wait_ge(mats_ready, 2 * (r + 1))
                for kh in range(2):
                    sp.dma_start(ap(mix_d, 8 * kh * C * 12 * C + (3 - r) * 3 * C, [[12 * C, C], [C * 12 * C, 8], [1, 3 * C]]),
                                 m_out[C * kh:C * kh + C, r % 2].rearrange("d k p e -> d k (p e)")).then_inc(mats_stored[r % 2], 16)
            sp.wait_ge(f_rows_stored, 16)
            for stored in mats_stored:
                sp.wait_ge(stored, 32 * BRANCHES // 2)
            for m, (n, j2s) in enumerate(PASSES):
                ncol = 2 + P * (n % NJ - j2s[0] + 1)
                seg0, nseg = unit_ranges(n % NJ)
                with sp.Fori(0, 2) as i:
                    for kk in range(8):
                        slot = kk % NSLOT
                        sp.wait_ge(filt_used[slot], START + 4 * m + 2 * i + kk // NSLOT)
                        k = 8 * i + kk
                        sp.dma_start(ring_h[:, slot].rearrange("s p h c -> s (p h) c")[:, :, 0:ncol],
                                     ap(hankel, k * 4 * HROW + HPAD - 2 - (P - 1), [[1, P], [HROW, 4], [1, ncol]])
                                     ).then_inc(filt_loaded[slot], 16)
                        sp.dma_start(ring_m[:, slot, 0:(3 * nseg - 1) * C],
                                     ap(mix_d, k * C * 12 * C + seg0 * 3 * C, [[C, 2], [12 * C, C], [1, (3 * nseg - 1) * C]])
                                     ).then_inc(filt_loaded[slot], 16)

        @block.gpsimd
        def _(pool):
            pool.memset(zeros[:], 0.0).then_inc(zeroed, 1)
            pool.memset(n_pad[:], 0.0)
            pool.memset(w_off[:], 0.0).then_inc(zeroed, 1)
            pool.memset(uT[:, :, :, 0:1], 0.0).then_inc(zeroed, 1)
            for bp in range(BP):
                pool.wait_ge(table_stored[bp], 16 * 4)
                with pool.Fori(0, NJ // 2) as i:
                    for h in range(2):
                        q = 4 * bp + 2 * i + h
                        pool.wait_ge(idx_ready, q + 1)
                        for k in range(BLK):
                            pool.wait_ge(v_ready[k % 2], START + 2 * q + k // 2 - 1)
                            pool.sem_inc(pool_marks, 1)
                            for tap in range(TAPS):
                                pool.indirect_dma_start(
                                    G[:, k, tap, :], None, table[bp],
                                    bass.IndirectOffsetOnAxis(ap=idx[:, h, k, tap:tap + 1], axis=0)
                                ).then_inc(gathered[k], 16)

        @block.vector
        def _(dve):
            steps = [0]

            def chain(ins):
                steps[0] += 1
                ins.then_inc(dve_step, 1)
                dve.wait_ge(dve_step, steps[0])

            def rsqrt(y, v, t):
                link(dve.tensor_scalar(t.bitcast(I32), v.bitcast(I32), 1, None, ALU.logical_shift_right))
                link(dve.tensor_scalar(y.bitcast(I32), t.bitcast(I32), -1.0, RSQRT_SEED, ALU.mult, ALU.add))
                for _ in range(3):
                    link(dve.scalar_tensor_tensor(t, y, -0.5, y, ALU.mult, ALU.mult))
                    link(dve.tensor_tensor(t, t, v, ALU.mult))
                    link(dve.scalar_tensor_tensor(y, t, 1.5, y, ALU.add, ALU.mult))

            link = chain

            for s in (*v_ready, y_used):
                dve.sem_inc(s, START)
            dve.memset(ones[:], 1.0)
            dve.memset(vT[C:C + 1, :, 4, :], 1.0)
            dve.memset(f_rows[:], 0.0)
            for bp in range(BP):
                dve.wait_ge(s_x[bp], 16)
                dve.tensor_copy(x_rev[:, bp, :], x_ch[:, bp, ::-1]).then_inc(x_reversed, 1)
            dve.wait_ge(s_woff, 32)
            raw = w_off_raw[:].rearrange("o (c t) -> o t c", t=TAPS)
            dve.tensor_copy(w_off_dup[:, :, 0, :], raw)
            dve.tensor_copy(w_off_dup[:, :, 1, :], raw).then_inc(woff_ready, 1)
            dve.wait_ge(s_const, 64)
            link(dve.tensor_tensor(grid[:], grid[:], off_bias[:].unsqueeze(1).broadcast_to([P, 8, NOFF]), ALU.subtract))
            for bp in range(BP):
                qs = slice(4 * bp, 4 * bp + 4)
                xs = x_tok[:, qs].rearrange("s q p b c -> s (q p b) c")
                ns = n_tok[:, qs].rearrange("s q p b c -> s (q p b) c")
                tmp = G[:, 2 * bp, 0:4, :].rearrange("s t r -> s (t r)").rearrange("s (g c) -> s g c", c=C)
                dve.wait_ge(x_copied, 2 * (bp + 1))
                link(dve.tensor_reduce(stat[:, 0, :], xs, AX.X, ALU.add))
                link(dve.tensor_scalar(stat[:, 1, :], stat[:, 0, :], 1.0 / C, None, ALU.mult))
                link(dve.tensor_tensor(ns, xs, stat[:, 1, :].unsqueeze(2).broadcast_to([P, 16, C]), ALU.subtract))
                link(dve.tensor_tensor(tmp, ns, ns, ALU.mult))
                link(dve.tensor_reduce(stat[:, 2, :], tmp, AX.X, ALU.add))
                link(dve.tensor_scalar(stat[:, 3, :], stat[:, 2, :], 1.0 / C, LN1_EPS, ALU.mult, ALU.add))
                rsqrt(stat[:, 4, :], stat[:, 3, :], stat[:, 5, :])
                link(dve.tensor_tensor(ns, ns, stat[:, 4, :].unsqueeze(2).broadcast_to([P, 16, C]), ALU.mult))
                for p in range(2):
                    last = dve.tensor_copy(n_store[:, qs, :, 1 - p, :], n_tok[:, qs, p])
                last.then_inc(n_ready, 1)

            def offsets(bp):
                dve.wait_ge(off_turned, bp + 1)
                for b2 in range(2):
                    dst = offs[:, 4 * bp:4 * bp + 4, b2::2, :].rearrange("s (g j) p n -> s g (j p) n", g=2)
                    src = off_ps[:, 256 * b2:256 * b2 + 256].rearrange("s (m g n) -> s g m n", m=4, g=2)
                    last = dve.tensor_tensor(dst, grid[:].rearrange("s (g m) n -> s g m n", g=2), src[:, :, :, 0:NOFF], ALU.subtract)
                last.then_inc(off_copied, 1)

            def masks(bp):
                m = mask[:, 4 * bp:4 * bp + 4].rearrange("s q k t -> s (q k t)")
                dve.wait_ge(mask_exp, bp + 1)
                link(dve.tensor_scalar(m, m, 1.0, None, ALU.add))
                link(dve.reciprocal(m, m))

            def positions(q, slot):
                o = offs[:, q] if isinstance(q, int) else offs[:, bass.ds(q, 1)].rearrange("s o k n -> s (o k) n")
                mk = mask[:, q] if isinstance(q, int) else mask[:, bass.ds(q, 1)].rearrange("s o k n -> s (o k) n")
                pk = pos[:].rearrange("s k t a -> s k (t a)")
                link(dve.tensor_scalar(pk, o[:, :, 0:2 * TAPS], 0.0, float(H + 1), ALU.max, ALU.min))
                link(dve.tensor_copy(pos_i[:], pos[:]))
                link(dve.tensor_tensor(corner[:], pos_i[:], pos[:], ALU.is_gt))
                link(dve.tensor_tensor(corner[:], pos_i[:], corner[:], ALU.subtract))
                link(dve.tensor_scalar(corner[:], corner[:], float(H), None, ALU.min))
                dve.tensor_tensor(frac[:], pos[:], corner[:], ALU.subtract)
                link(dve.scalar_tensor_tensor(idx_f[:], corner[:, :, :, 0], float(SIDE), corner[:, :, :, 1], ALU.mult, ALU.add))
                dve.tensor_tensor(idx[:, slot], idx_f[:], first_row[:].unsqueeze(2).broadcast_to([P, BLK, TAPS]), ALU.add
                                  ).then_inc(idx_ready, 1)
                link(dve.tensor_scalar(anti[:], frac[:], -1.0, 1.0, ALU.mult, ALU.add))
                dve.tensor_tensor(my[:, 0], mk, anti[:, :, :, 0], ALU.mult)
                link(dve.tensor_tensor(my[:, 1], mk, frac[:, :, :, 0], ALU.mult))
                for cy in range(2):
                    dve.tensor_tensor(wts[:, slot, :, :, 2 * cy], my[:, cy], anti[:, :, :, 1], ALU.mult)
                    last = dve.tensor_tensor(wts[:, slot, :, :, 2 * cy + 1], my[:, cy], frac[:, :, :, 1], ALU.mult)
                link(last)

            dve.wait_ge(s_small, 16 * N_SMALL)
            link(dve.tensor_tensor(br[:, 2, :], br[:, 0, :], br[:, 1, :], ALU.add))
            link(dve.tensor_reduce(br[:, 3, 0:1], br[:, 2, :], AX.X, ALU.max))
            dve.tensor_scalar(br[:, 4, :], br[:, 2, :], br[:, 3, 0:1], None, ALU.subtract).then_inc(br_ready, 1)
            for r in range(BRANCHES):
                dve.memset(br[:, 8, r:r + 1], float(BRANCHES - r))
            rsqrt(sig[:, 1, :], sig[:, 0, :], sig[:, 2, :])
            link(dve.tensor_tensor(sig[:, 1, :], sig[:, 1, :], sig[:, 0, :], ALU.mult))
            rsqrt(sig[:, 3, :], sig[:, 1, :], sig[:, 2, :])
            link(dve.tensor_tensor(sig[:, 3, :], sig[:, 3, :], sig[:, 1, :], ALU.mult))
            dve.wait_ge(s_bn, 16 * 6)
            bn = bn_row[C:C + 1]
            tmp = expo[C:C + 1]
            link(dve.tensor_scalar(bn[:, 3, :], bn[:, 3, :], BN_EPS, None, ALU.add))
            rsqrt(tmp[:, 0, :], bn[:, 3, :], tmp[:, 1, :])
            link(dve.tensor_tensor(bn[:, 0, :], bn[:, 0, :], tmp[:, 0, :], ALU.mult))
            link(dve.tensor_tensor(bn[:, 2, :], bn[:, 2, :], bn[:, 0, :], ALU.mult))
            dve.tensor_tensor(w_main[C:C + 1, 4, :], bn[:, 1, :], bn[:, 2, :], ALU.subtract).then_inc(w_ready, 1)
            offsets(0)
            masks(0)
            positions(0, 0)
            dve.wait_ge(br_exp, 1)
            link(dve.reciprocal(br[:, 3, 2:3], br[:, 3, 1:2]))
            link(dve.tensor_scalar(br[:, 6, :], br[:, 5, :], br[:, 3, 2:3], None, ALU.mult))
            link(dve.tensor_reduce(br[:, 3, 3:4], br[:, 6, :], AX.X, ALU.max))
            link(dve.scalar_tensor_tensor(br[:, 7, :], br[:, 6, :], br[:, 3, 3:4], br[:, 8, :], ALU.is_ge, ALU.mult))
            link(dve.tensor_reduce(br[:, 3, 0:1], br[:, 7, :], AX.X, ALU.max))
            link(dve.tensor_scalar(br[:, 7, :], br[:, 7, :], br[:, 3, 0:1], None, ALU.is_equal))
            link(dve.tensor_tensor(br[:, 7, :], br[:, 7, :], br[:, 6, :], ALU.subtract))
            link(dve.tensor_tensor(br[:, 9, :], br[:, 7, :], br[:, 6, :], ALU.add))
            for r in range(BRANCHES):
                for sign in range(2):
                    last = dve.tensor_scalar(w_diag[:, r, sign, :], ident, br[:, 9, r:r + 1], 1.0 - 2.0 * sign, ALU.mult, ALU.mult)
            last.then_inc(w_diag_ready, 1)
            dve.wait_ge(s_w, 16)
            dve.wait_ge(s_bn, 16 * 6)
            link(dve.tensor_scalar(bn_col[:, 1:2], bn_col[:, 1:2], BN_EPS, None, ALU.add))
            rsqrt(st2[0:C, 0, 0:1], bn_col[:, 1:2], st2[0:C, 1, 0:1])
            link(dve.tensor_tensor(bn_col[:, 0:1], bn_col[:, 0:1], st2[0:C, 0, 0:1], ALU.mult))
            dve.tensor_scalar(w_scaled[:].rearrange("o (t c) -> o t c", t=TAPS),
                              w_raw[:].rearrange("o (c t) -> o t c", t=TAPS), bn_col[:, 0:1], None, ALU.mult
                              ).then_inc(w_ready, 1)

            dve.wait_ge(phi_turned, 1)
            for par in range(2):
                last = dve.tensor_reduce(f_max[:, 2 + par:3 + par], val_ps[par][0:K, :], AX.X, ALU.max, apply_absolute_value=True)
            link(last)
            link(dve.tensor_tensor(f_max[:, 0:1], f_max[:, 2:3], f_max[:, 3:4], ALU.max))
            link(dve.tensor_scalar(f_max[:, 0:1], f_max[:, 0:1], 1e-30, 1.0 / PHI_SCALE, ALU.max, ALU.mult))
            link(dve.reciprocal(f_max[:, 1:2], f_max[:, 0:1]))
            for par in range(2):
                row = f_rows[:, par, :, HPAD:HPAD + HALF]
                link(dve.tensor_scalar(row[:, 0, :], val_ps[par][0:K, :], f_max[:, 1:2], None, ALU.mult))
                last = dve.scalar_tensor_tensor(row[:, 1, :], val_ps[par][0:K, :], f_max[:, 1:2], row[:, 0, :], ALU.mult, ALU.subtract)
            last.then_inc(f_rows_ready, 1)
            link(dve.reciprocal(f_max[:, 2:3], f_max[:, 1:2]))
            dve.tensor_scalar(f_diag[:], ident[0:K, 0:K], f_max[:, 2:3], None, ALU.mult).then_inc(diag_ready, 1)


            def weigh(q, slot, p, b2):
                k = 2 * p + b2
                dve.wait_ge(gathered[k], 16 * TAPS * (q + 1))
                g = G[:, k].rearrange("s t (n c) -> s (t n) c", c=C)
                w = wts[:, slot, k].rearrange("s t n -> s (t n)").unsqueeze(2).broadcast_to([P, 4 * TAPS, C])
                link(dve.tensor_tensor(g, g, w, ALU.mult))
                link(dve.tensor_tensor(G[:, k, :, 0:2 * C], G[:, k, :, 0:2 * C], G[:, k, :, 2 * C:4 * C], ALU.add))
                if b2 == 0:
                    dve.wait_ge(val_turned, START + 2 * q + p)
                dve.tensor_tensor(V[:, b2].rearrange("s (t c) -> s t c", c=C), G[:, k, :, 0:C], G[:, k, :, C:2 * C], ALU.add
                                  ).then_inc(v_ready[b2], 1)

            def finish(q, p):
                r = 2 * q + p
                xs = x_tok[:, bass.ds(q, 1), p].rearrange("s o b c -> s (o b) c")
                x2 = x2_tok[:, bass.ds(r, 1)].rearrange("s o b c -> s (o b) c")
                hi = u_hi[:, bass.ds(q, 1), :, p].rearrange("s o b c -> s (o b) c")
                lo = u_lo[:, bass.ds(q, 1), :, p].rearrange("s o b c -> s (o b) c")
                u = u_tok[:].rearrange("s (b c) -> s b c", b=2)
                dve.wait_ge(y_exp, r + 1)
                link(dve.tensor_scalar(expo[:], expo[:], 1.0, None, ALU.add))
                link(dve.reciprocal(sil[:], expo[:]))
                dve.tensor_tensor(sil[:], y_ps.rearrange("s (b c) -> s b c", b=2), sil[:], ALU.mult).then_inc(y_used, 1)
                dve.wait_ge(y_used, START + r + 1)
                link(dve.tensor_tensor(x2, xs, sil[:], ALU.add))
                dve.sem_inc(dve_marks, 1)
                link(dve.tensor_reduce(st2[:, 0, :], x2, AX.X, ALU.add))
                link(dve.tensor_scalar(st2[:, 1, :], st2[:, 0, :], 1.0 / C, None, ALU.mult))
                link(dve.tensor_tensor(cen[:], x2, st2[:, 1, :].unsqueeze(2).broadcast_to([P, 2, C]), ALU.subtract))
                link(dve.tensor_tensor(sq[:], cen[:], cen[:], ALU.mult))
                link(dve.tensor_reduce(st2[:, 2, :], sq[:], AX.X, ALU.add))
                link(dve.tensor_scalar(st2[:, 3, :], st2[:, 2, :], 1.0 / C, LN2_EPS, ALU.mult, ALU.add))
                rsqrt(st2[:, 4, :], st2[:, 3, :], st2[:, 5, :])
                dve.wait_ge(u_turned, START + r)
                link(dve.tensor_tensor(u, cen[:],
                                       st2[:, 4, :].unsqueeze(2).broadcast_to([P, 2, C]), ALU.mult))
                link(dve.tensor_scalar(hi, u, U_SCALE, None, ALU.mult))
                dve.scalar_tensor_tensor(lo, u, U_SCALE, hi, ALU.mult, ALU.subtract).then_inc(u_ready, 1)

            def quarter(q, slot):
                positions(q + 1, 1 - slot)
                weigh(q, slot, 1, 0)
                finish(q, 0)
                weigh(q, slot, 1, 1)
                weigh(q + 1, 1 - slot, 0, 0)
                finish(q, 1)
                weigh(q + 1, 1 - slot, 0, 1)

            weigh(0, 0, 0, 0)
            weigh(0, 0, 0, 1)
            dve.wait_ge(f_scale_ready, 1)
            dve.scalar_tensor_tensor(f_scale[:], bank[3][:, 0:K], 1.0 / U_SCALE, sig[:, 3, :], ALU.mult, ALU.mult
                                     ).then_inc(f_scale_done, 1)
            positions(1, 1)
            weigh(0, 0, 1, 0)
            finish(0, 0)
            weigh(0, 0, 1, 1)
            offsets(1)
            masks(1)
            finish(0, 1)
            weigh(1, 1, 0, 0)
            weigh(1, 1, 0, 1)
            per_loop = LINKS_PER_QUARTER * 2
            with dve.Fori(0, NQ // 2 - 1) as i:
                at0 = steps[0]

                def link(ins, i=i, at0=at0):
                    steps[0] += 1
                    ins.then_inc(dve_step, 1)
                    dve.wait_ge(dve_step, steps[0] + per_loop * i)
                quarter(2 * i + 1, 1)
                quarter(2 * i + 2, 0)
                assert steps[0] - at0 == per_loop, (steps[0] - at0)
            steps[0] += per_loop * (NQ // 2 - 2)
            link = chain
            weigh(NQ - 1, 1, 1, 0)
            finish(NQ - 1, 0)
            weigh(NQ - 1, 1, 1, 1)
            finish(NQ - 1, 1)

        @block.scalar
        def _(act):
            act.dma_start(w_raw[:], ap(weight, 0, [[C * TAPS, C], [1, C * TAPS]])).then_inc(s_w, 16)
            for i, v in enumerate((gamma, var)):
                act.dma_start(bn_col[:, i:i + 1], ap(v, 0, [[1, C], [1, 1]])).then_inc(s_bn, 16)
            for i, v in enumerate((gamma, beta, mean, var)):
                act.dma_start(bn_row[C:C + 1, i, :], ap(v, 0, [[C, 1], [1, C]])).then_inc(s_bn, 16)
            for s in (u_copied, *conv_copied):
                act.sem_inc(s, START)
            for g in range(4):
                bp, jj = divmod(g, 2)
                act.wait_ge(x_turned, g + 1)
                act.copy(x_tok[:, 4 * bp + 2 * jj:4 * bp + 2 * jj + 2].rearrange("s q p b c -> s (q p b c)"),
                         bank[g][:]).then_inc(x_copied, 1)
            act.wait_ge(woff_turned, 1)
            act.wait_ge(zeroed, 2)
            act.copy(w_off[:, :, 0:NOFF], bank[6][:, 0:TAPS * NOFF].rearrange("c (t n) -> c t n", t=TAPS)).then_inc(woff_copied, 1)

            def lay_out_normalised(bp):
                for jj in range(2):
                    act.wait_ge(n_turned, 2 * bp + jj + 1)
                    for p in range(2):
                        last = act.copy(n_pad[:, bp, 17 - 16 * jj:33 - 16 * jj, 2 - p:2 - p + W - 1:2],
                                        bank[2 + jj][:, 256 * p:256 * p + 256].rearrange("c (y x) -> c y x", x=16))
                    last.then_inc(n_copied, 1)

            def lay_out_offsets(bp):
                act.wait_ge(off_done, bp + 1)
                if bp:
                    act.wait_ge(off_turned, bp)
                act.copy(off_ch[:, 0, :], bank[0][:])
                act.copy(off_ch[:, 1, :], bank[1][:]).then_inc(off_laid, 1)

            def exp_masks(bp):
                act.wait_ge(off_copied, bp + 1)
                qs = slice(4 * bp, 4 * bp + 4)
                act.activation(mask[:, qs].rearrange("s q k t -> s (q k) t"),
                               offs[:, qs].rearrange("s q k n -> s (q k) n")[:, :, 2 * TAPS:NOFF], ACT.Exp).then_inc(mask_exp, 1)

            lay_out_normalised(0)
            act.wait_ge(br_ready, 1)
            act.activation(br[:, 5, :], br[:, 4, :], ACT.Exp, accum_out=br[:, 3, 1:2]).then_inc(br_exp, 1)
            lay_out_offsets(0)
            exp_masks(0)
            lay_out_normalised(1)
            lay_out_offsets(1)
            act.wait_ge(w_turned, 1)
            act.copy(w_main[:, 0:4, :], bank[6][:, 0:4 * C].rearrange("k (t o) -> k t o", t=4))
            act.copy(w_main[0:C, 4, :], bank[6][0:C, 4 * C:5 * C]).then_inc(w_copied, 1)
            for r in range(BRANCHES):
                for par in range(2):
                    act.wait_ge(mats_summed, 3 * r + par + 1)
                    if par == 0 and r >= 2:
                        act.wait_ge(mats_stored[r % 2], 32)
                    sums = bank[par][:].rearrange("d (k e) -> d k e", k=8)
                    if par == 0:
                        act.copy(m_out[:, r % 2, :, 2, :], sums)
                    act.copy(m_out[:, r % 2, :, par, :], sums).then_inc(mats_ready, 1)
                act.wait_ge(mats_summed, 3 * r + 3)
                act.copy(mu[:, 3 - r].rearrange("d i e -> d (i e)"), bank[2][:, 0:3 * C]).then_inc(mu_ready, 1)

            def copy_values(r):
                act.wait_ge(val_turned, START + r + 1)
                for b2 in range(2):
                    act.copy(vT[:, b2, 0:4, :], val_ps[b2][:].rearrange("k (m s) -> k m s", m=4))
                act.copy(vT[0:C, :, 4, :], tail_ps[0:C, 0:256].rearrange("k (b s) -> k b s", b=2)).then_inc(val_copied, 1)

            def exp_y(r):
                act.wait_ge(y_done, r + 1)
                act.wait_ge(y_used, START + r)
                act.activation(expo[:], y_ps.rearrange("s (b c) -> s b c", b=2), ACT.Exp, scale=-1.0).then_inc(y_exp, 1)

            def copy_tokens(q, i):
                act.wait_ge(u_turned, START + 2 * q + i + 1)
                act.copy(uT[:, bass.ds(i, 1), q // NJ, 1 + P * (q % NJ):1 + P * (q % NJ) + P].rearrange("c o a -> c (o a)"),
                         val_ps[0][:, 0:P]).then_inc(u_copied, 1)

            copy_values(0)
            exp_y(0)
            copy_tokens(0, 0)
            copy_values(1)
            exp_masks(1)
            exp_y(1)
            copy_tokens(0, 1)
            act.wait_ge(f_scale_done, 1)

            def copy_products(m, kk, i):
                for b2 in range(2):
                    act.wait_ge(conv_done[b2], 16 * m + 8 * i + kk + 1)
                    act.sem_inc(act_marks, 1)
                    for src in range(2):
                        half = slice(C * src, C * src + C)
                        c = conv_ps[b2][half, :]
                        first, stride = ((1, NCOL), (NCOL, 1 - NCOL))[src]
                        c = bass.AP(c.tensor, c.offset + first, [c.ap[0], [stride, 2], [1, P]])
                        last = act.activation(u_conv[half, kk % 2, b2], c, ACT.Copy, scale=f_scale[half, bass.ds(8 * i + kk, 1)])
                    last.then_inc(conv_copied[b2], 1)

            for m, (n, j2s) in enumerate(PASSES):
                def half_pass(i):
                    r = hosted(m, i)
                    for kk in range(8):
                        copy_products(m, kk, i)
                        if r is not None and kk == VALUES_AT:
                            copy_values(r)
                        if r is not None and kk == Y_AT:
                            exp_y(r)
                        if r is not None and kk == TOKENS_AT:
                            copy_tokens(n + 1, i)

                run_halves(act, m, half_pass)
                if j2s[-1] == n % NJ:
                    act.wait_ge(filt_used[NSLOT - 1], START + 4 * (m + 1))
                    if n >= 2:
                        act.wait_ge(out_stored[n % 2], 16 * (n // 2))
                    act.copy(o_sb[:, n % 2, :].rearrange("e (a p) -> e p a", p=2),
                             acc_ps[n % 2][:, 0:2 * P].rearrange("e (p a) -> e p a", p=2)).then_inc(out_copied, 1)
                    act.wait_ge(out_copied, n + 1)
                    act.dma_start(ap(out, (n // NJ) * 2 * C * T + 2 * P * (n % NJ), [[T, P], [1, 2 * P]]),
                                  o_sb[:, n % 2, :]).then_inc(out_stored[n % 2], 16)
            for stored in out_stored:
                act.wait_ge(stored, 16 * NQ // 2)

        @block.tensor
        def _(pe):
            for s in (val_turned, u_turned, *filt_used):
                pe.sem_inc(s, START)
            pe.wait_ge(s_ident, 16)
            for g in range(4):
                bp, jj = divmod(g, 2)
                if jj == 0:
                    pe.wait_ge(x_reversed, bp + 1)
                for j2 in range(2):
                    for p in range(2):
                        t = T - 255 - 256 * (2 * jj + j2) - p
                        last = pe.transpose(bank[g][:, P * (2 * j2 + p):P * (2 * j2 + p) + P], x_rev[:, bp, t:t + 255:2], ident)
                last.then_inc(x_turned, 1)
            pe.wait_ge(woff_ready, 1)
            for t in range(TAPS):
                last = pe.transpose(bank[6][:, NOFF * t:NOFF * t + NOFF], w_off_dup[:, t].rearrange("o h c -> o (h c)"),
                                    ident[0:NOFF, 0:NOFF])
            last.then_inc(woff_turned, 1)

            def keep_warm(n):
                for _ in range(n):
                    pe.matmul(bank[6][:], ident, x_ch[:, 0, 0:512], start=True, stop=True)

            def turn_normalised(bp):
                pe.wait_ge(n_ready, bp + 1)
                pe.wait_ge(x_copied, 4)
                for jj in range(2):
                    for j2 in range(2):
                        for p in range(2):
                            last = pe.transpose(bank[2 + jj][:, 256 * p + P * (1 - j2):256 * p + P * (1 - j2) + P],
                                                n_tok[:, 4 * bp + 2 * jj + j2, p].rearrange("s b c -> s (b c)"), ident)
                    last.then_inc(n_turned, 1)

            def convolve_offsets(bp):
                pe.wait_ge(n_copied, 2 * (bp + 1))
                if bp:
                    pe.wait_ge(off_laid, bp)
                pe.wait_ge(woff_copied, 1)
                for t in range(len(TAP_HALVES[0])):
                    for b2 in range(2):
                        for tg in range(2):
                            if t == len(TAP_HALVES[tg]):
                                continue
                            tap = TAP_HALVES[tg][t]
                            dy, dx = divmod(tap, 3)
                            for jj in range(2):
                                half = slice(C * b2, C * b2 + C)
                                y0, x0 = 18 - 16 * jj - dy, 2 - dx
                                a = n_pad[half, bp, y0:y0 + 16, x0:x0 + W - 1:2]
                                a = bass.AP(a.tensor, a.offset, [a.ap[0], [1, 2], *a.ap[1:]])
                                group = NCH * (2 * tg + jj)
                                last = pe.matmul(bank[b2][group:group + NCH, :], w_off[half, tap, :], a,
                                                 start=(t == 0), stop=(tap == TAP_HALVES[tg][-1]))
                last.then_inc(off_done, 1)

            def turn_offsets(bp):
                pe.wait_ge(off_laid, bp + 1)
                if bp:
                    pe.wait_ge(off_copied, bp)
                for b2 in range(2):
                    for j2 in range(2):
                        for p in range(2):
                            col = 64 * (4 * b2 + 2 * j2 + p)
                            src = 256 * (1 - p) + P * (1 - j2)
                            last = pe.matmul(off_ps[:, col:col + 64], off_ch[:, b2, src:src + P], fold, start=True, stop=True)
                last.then_inc(off_turned, 1)

            pe.wait_ge(woff_copied, 1)
            keep_warm(WARM_UP)
            turn_normalised(0)
            keep_warm(1)
            convolve_offsets(0)
            turn_offsets(0)
            turn_normalised(1)
            pe.wait_ge(s_phi, 16)
            for par in range(2):
                for j in range(NJ):
                    last = pe.transpose(val_ps[par][0:K, P * j:P * j + P], phi_sb[:, j, par, :], ident)
            last.then_inc(phi_turned, 1)
            keep_warm(1)
            convolve_offsets(1)
            turn_offsets(1)
            pe.wait_ge(w_ready, 2)
            for m in range(5):
                rows = min(P, (TAPS - 2 * m) * C)
                last = pe.transpose(bank[6][0:rows, C * m:C * m + C], w_scaled[:, P * m:P * m + rows], ident[0:C, 0:C])
            last.then_inc(w_turned, 1)
            pe.wait_ge(off_laid, 2)
            pe.wait_ge(w_diag_ready, 1)
            pe.wait_ge(s_mats, 16 * 6 * BRANCHES)
            for r in range(BRANCHES):
                for par in range(2):
                    if r:
                        pe.wait_ge(mats_ready, 2 * r - 1 + par)
                    pe.matmul(bank[par][:], w_diag[:, r, 0, :], m_raw[:, r, 0].rearrange("d k e -> d (k e)"),
                              start=(r == 0), stop=False, skip_group_check=True)
                    pe.matmul(bank[par][:], w_diag[:, r, par, :], m_raw[:, r, 1].rearrange("d k e -> d (k e)"),
                              start=False, stop=(r == BRANCHES - 1), skip_group_check=True).then_inc(mats_summed, 1)
                if r:
                    pe.wait_ge(mu_ready, r)
                pe.matmul(bank[2][:, 0:3 * C], w_diag[:, r, 0, :], mu_raw[:, r, :], start=(r == 0),
                          stop=(r == BRANCHES - 1), skip_group_check=True).then_inc(mats_summed, 1)

            pe.wait_ge(diag_ready, 1)
            pe.matmul(bank[3][:, 0:K], ones[:], f_diag[:], start=True, stop=True).then_inc(f_scale_ready, 1)

            def turn_values(r):
                for b2 in range(2):
                    pe.wait_ge(v_ready[b2], START + r + 1)
                pe.wait_ge(y_used, START + r)
                pe.wait_ge(u_copied, START + r)
                for b2 in range(2):
                    for m in range(4):
                        pe.transpose(val_ps[b2][:, P * m:P * m + P], V[:, b2, P * m:P * m + P], ident)
                    last = pe.transpose(tail_ps[0:C, P * b2:P * b2 + P], V[:, b2, 4 * P:4 * P + C], ident)
                last.then_inc(val_turned, 1)

            def convolve_values(r):
                pe.wait_ge(val_copied, r + 1)
                for b2 in range(2):
                    for m in range(5):
                        rows = min(P, (TAPS - 2 * m) * C + 1)
                        last = pe.matmul(y_ps[:, C * b2:C * b2 + C], vT[0:rows, b2, m, :], w_main[0:rows, m, :],
                                         start=(m == 0), stop=(m == 4))
                last.then_inc(y_done, 1)

            def turn_tokens(r):
                pe.wait_ge(u_ready, r + 1)
                pe.matmul(val_ps[0][:, 0:P], u_tok[:], swap, start=True, stop=True).then_inc(u_turned, 1)

            pe.wait_ge(w_copied, 1)
            pe.wait_ge(zeroed, 3)
            turn_values(0)
            convolve_values(0)
            turn_tokens(0)
            turn_values(1)
            convolve_values(1)
            for _ in range(WARM_UP_UNITS):
                pe.matmul(bank[1][:], ident, x_both[:, 3072:3584], start=True, stop=True)
            turn_tokens(1)

            for m, (n, j2s) in enumerate(PASSES):
                bp, j = divmod(n, NJ)
                seg0, nseg = unit_ranges(j)
                acc = acc_ps[n % 2]
                opens, closes = j2s[0] == 0, j2s[-1] == j
                ranges = [(s, max(SEGS[s][0], P * j) - P * j, min(SEGS[s][1], P * j + P) - P * j)
                          for s in range(seg0, seg0 + nseg)]

                def convolve(kk, i):
                    slot = kk % NSLOT
                    pe.wait_ge(filt_loaded[slot], 32 * (4 * m + 2 * i + kk // NSLOT + 1))
                    for b2 in range(2):
                        pe.wait_ge(conv_copied[b2], START + 16 * m + 8 * i + kk)
                        for j2 in j2s:
                            c0 = 1 + P * (j - j2)
                            for e, (u, part) in enumerate(((u_hi, 0), (u_hi, 1), (u_lo, 0))):
                                h = ring_h[:, slot, :, part, c0:c0 + NCOL]
                                last = pe.matmul(conv_ps[b2][:, 0:2 * NCOL].rearrange("c (t a) -> c t a", t=2),
                                                 u[:, NJ * bp + j2, b2].rearrange("s p c -> s (p c)"), h,
                                                 start=(j2 == j2s[0] and e == 0), stop=(j2 == j2s[-1] and e == 2))
                        last.then_inc(conv_done[b2], 1)

                def mix(kk, i):
                    slot = kk % NSLOT
                    for b2 in range(2):
                        pe.wait_ge(conv_copied[b2], START + 16 * m + 8 * i + kk + 1)
                    pe.sem_inc(pe_marks, 1)
                    start = not closes and kk == 0 and isinstance(i, int) and i == 0
                    for s, a0, a1 in ranges:
                        for p in range(2):
                            for b2 in range(2):
                                first = ((s - seg0) * 3 + p) * C
                                last = pe.matmul(acc[C * b2:C * b2 + C, P * p + a0:P * p + a1], ring_m[:, slot, first:first + C],
                                                 u_conv[:, kk % 2, b2, p, a0:a1], start=start and p == 0, stop=False,
                                                 skip_group_check=True)
                    last.then_inc(filt_used[slot], 1)

                if opens and n >= 2:
                    pe.wait_ge(out_copied, n - 1)
                if closes:
                    pe.wait_ge(u_copied, START + 2 * n + 2)
                    for p in range(2):
                        pe.matmul(acc[:, P * p:P * p + P], x2_tok[:, 2 * n + p].rearrange("s b c -> s (b c)"), swap,
                                  start=opens and p == 0, stop=False, skip_group_check=True)
                    for lag in range(3):
                        (src, shift), (src1, shift1) = [((p - lag) % 2, (p - lag) // 2) for p in range(2)]
                        for s, a0, a1 in ranges:
                            for b2 in range(2):
                                half = slice(C * b2, C * b2 + C)
                                u = uT[half, src, bp, 1 + P * j + shift + a0:1 + P * j + shift + a1]
                                u = bass.AP(u.tensor, u.offset, [u.ap[0], [(src1 - src) * BP * (1 + HALF) + shift1 - shift, 2], u.ap[-1]])
                                pe.matmul(acc[half, 0:2 * P].rearrange("e (p a) -> e p a", p=2)[:, :, a0:a1], mu[half, s, lag, :], u,
                                          start=False, stop=False, skip_group_check=True)

                def half_pass(i):
                    r = hosted(m, i)
                    for kk in range(8):
                        convolve(kk, i)
                        if kk:
                            mix(kk - 1, i)
                        if r is not None and kk == VALUES_AT:
                            turn_values(r)
                        if r is not None and kk == Y_AT:
                            convolve_values(r)
                        if r is not None and kk == TOKENS_AT:
                            turn_tokens(r)
                    mix(7, i)

                run_halves(pe, m, half_pass)


LINKS_PER_QUARTER = 61
VALUES_AT, Y_AT, TOKENS_AT = 1, 3, 7


def hosted(m, i):
    return 2 * m + 2 + i if m < NQ - 1 else None


def run_halves(engine, m, body):
    if m < NQ:
        with engine.Fori(0, 2) as i:
            body(i)
    else:
        for i in range(2):
            body(i)


def unit_ranges(j):
    hit = [s for s, (a, b) in enumerate(SEGS) if a < P * (j + 1) and b > P * j]
    return hit[0], len(hit)


_INS = ['x', 'L0_conv_offset_w', 'L0_conv_offset_b', 'L0_conv_mask_w', 'L0_conv_mask_b', 'L0_conv_weight',
        'L0_conv_bn_gamma', 'L0_conv_bn_beta', 'L0_conv_bn_mean', 'L0_conv_bn_var', 'L0_ffn_sigma', 'L0_ffn_phi',
        'L0_ffn_M_u', 'L0_ffn_M_phi_plus', 'L0_ffn_M_phi_minus', 'L0_ffn_log_weights', 'L0_ffn_gumbel']


def constants():
    s = P - 1 - np.arange(P)
    grid = np.zeros((P, 2 * NJ, NOFF), np.float32)
    for j in range(NJ):
        for p in range(2):
            for t in range(TAPS):
                grid[:, 2 * j + p, 2 * t] = H + 1 - (8 * j + s // 16 + t // 3)
                grid[:, 2 * j + p, 2 * t + 1] = W + 1 - (2 * (s % 16) + p + t % 3)
    first = np.array([k % 2 * SIDE * SIDE for k in range(BLK)], np.float32)
    return {"ident": np.stack([np.eye(P), np.eye(P)[::-1], np.tile(np.eye(C), (2, 2))], 1).astype(np.float32), "grid": grid, "first_row": np.tile(first, (P, 1))}


def kernel(**inputs):
    import numpy as _np
    import concourse.bacc as _bacc
    from concourse import mybir as _mybir
    from concourse.bass_utils import run_bass_kernel_spmd as _run

    nc = _bacc.Bacc("TRN2", target_bir_lowering=False, num_devices=1)
    arrays, args = {}, []
    for name, a in [(n, inputs[n]) for n in _INS] + list(constants().items()):
        a = _np.ascontiguousarray(a)
        arrays[f"in_{name}_dram"] = a
        args.append(nc.dram_tensor(f"in_{name}_dram", a.shape, _mybir.dt.from_np(a.dtype), kind="ExternalInput").ap())
    args.append(nc.dram_tensor("out_0_dram", (B, C, H, W), _mybir.dt.float32, kind="ExternalOutput").ap())
    metaformer_kernel(nc, *args)
    r = _run(nc, [arrays], core_ids=[0])
    return r.results[0]["out_0_dram"]
```

```python
import numpy as np
import concourse.bass as bass
from concourse import mybir
from contextlib import ExitStack

F32, F16, I32 = mybir.dt.float32, mybir.dt.float16, mybir.dt.int32
ALU, ACT, AX = mybir.AluOpType, mybir.ActivationFunctionType, mybir.AxisListType

P = 128
B, C, H, W = 4, 64, 32, 32
T = H * W
BP = B // 2
NJ = T // (2 * P)
NQ = BP * NJ
NR = 2 * NQ
BLK = 4
TAPS = 9
NOFF = 3 * TAPS
NCH = 32
ROW = 4 * C
SIDE = H + 1
PH, PW = H + 2, W + 2
K = 16
HALF = T // 2
BRANCHES = 4
HLEN = HALF + 2
HPAD = P + 2
HROW = HPAD + HALF + 2
START = 2
LN1_EPS, LN2_EPS, BN_EPS = 1e-6, 1e-5, 1e-5
U_SCALE = 32.0
PHI_SCALE = 256.0
NSLOT = 4
SEGS = [(0, HALF // 8), (HALF // 8, HALF // 4), (HALF // 4, HALF // 2), (HALF // 2, HALF)]
RSQRT_SEED = float(0x5F3759DF)
TAP_HALVES = (range(0, 5), range(5, 9))
NCOL = P + 1
WARM_UP, WARM_UP_UNITS = 9, 6


def metaformer_kernel(nc, x, offset_w, offset_b, mask_w, mask_b, weight, gamma, beta, mean, var,
                      sigma, phi, m_u, m_plus, m_minus, log_weights, gumbel, ident_in, grid_in, first_row_in, out):
    ctx = ExitStack()
    with ctx:
        def sb(name, shape, dt=F32):
            return ctx.enter_context(nc.sbuf_tensor(name, shape, dt))

        def sem(name):
            return ctx.enter_context(nc.semaphore(name))

        def dram(name, shape, dt=F32):
            return nc.dram_tensor(name, shape, dt, kind="Internal").ap()

        def ap(a, offset, dims):
            return bass.AP(a.tensor, offset, dims)

        padded = dram("padded", [B, PH, PW, C])
        table = [dram(f"corner_table{i}", [2 * SIDE * SIDE, ROW]) for i in range(BP)]
        hankel = dram("filter_rows", [K, 4, HROW], F16)
        mix_d = dram("mix_matrices", [K, C, 4, 3, C])

        ident_swap = sb("ident_swap", [P, 3, P])
        ident, swap = ident_swap[:, 0, :], ident_swap[:, 1, :]
        fold = ident_swap[:, 2, 0:C]
        grid = sb("grid", [P, 8, NOFF])
        first_row = sb("first_row", [P, BLK])
        zeros = sb("zeros", [P, PW * C // 16])
        ones = sb("ones", [K, P])
        off_bias = sb("off_bias", [P, NOFF])
        w_off_raw = sb("w_off_raw", [NOFF, C * TAPS])
        w_off_dup = sb("w_off_dup", [NOFF, TAPS, 2, C])
        w_off = sb("w_off", [P, TAPS, NCH])
        w_raw = sb("w_raw", [C, C * TAPS])
        w_scaled = sb("w_scaled", [C, TAPS * C])
        w_main = sb("w_main", [P, 5, C])
        bn_col = sb("bn_col", [C, 2])
        bn_row = sb("bn_row", [P, 4, C])
        x_both = sb("x_both", [P, 2 * BP * T])
        x_ch = x_both[:, 0:BP * T].rearrange("c (b t) -> c b t", b=BP)
        x_rev = x_both[:, BP * T:2 * BP * T].rearrange("c (b t) -> c b t", b=BP)
        x_tok = sb("x_tok", [P, NQ, 2, 2, C])
        n_tok = sb("n_tok", [P, NQ, 2, 2, C])
        n_pad = sb("n_pad", [P, BP, PH, PW])
        stat = sb("stat", [P, 6, 16])
        off_ch = sb("off_ch", [P, 2, 512])
        offs = sb("offs", [P, NQ, BLK, NOFF])
        mask = sb("mask", [P, NQ, BLK, TAPS])
        pos = sb("pos", [P, BLK, TAPS, 2])
        pos_i = sb("pos_i", [P, BLK, TAPS, 2], I32)
        corner = sb("corner", [P, BLK, TAPS, 2])
        frac = sb("frac", [P, BLK, TAPS, 2])
        anti = sb("anti", [P, BLK, TAPS, 2])
        my = sb("my", [P, 2, BLK, TAPS])
        idx_f = sb("idx_f", [P, BLK, TAPS])
        idx = sb("idx", [P, 2, BLK, TAPS], I32)
        wts = sb("wts", [P, 2, BLK, TAPS, 4])
        G = sb("G", [P, BLK, TAPS, ROW])
        V = sb("V", [P, 2, TAPS * C])
        n_store = sb("n_store", [P, NQ, 2, 2, C])
        vT = sb("vT", [P, 2, 5, P])
        y_chan = sb("y_chan", [P, P])
        expo = sb("expo", [P, 2, C])
        sil = sb("sil", [P, 2, C])
        cen = sb("cen", [P, 2, C])
        sq = sb("sq", [P, 2, C])
        st2 = sb("st2", [P, 6, 2])
        x2_tok = sb("x2_tok", [P, NR, 2, C])
        u_tok = sb("u_tok", [P, 2 * C])
        u_hi = sb("u_hi", [P, NQ, 2, 2, C], F16)
        u_lo = sb("u_lo", [P, NQ, 2, 2, C], F16)
        uT = sb("uT", [P, 2, BP, 1 + HALF])
        phi_sb = sb("phi_sb", [P, NJ, 2, K])
        f_max = sb("f_max", [K, 4])
        f_rows = sb("f_rows", [K, 2, 2, HROW], F16)
        f_diag = sb("f_diag", [K, K])
        sig = sb("sig", [P, 4, K])
        f_scale = sb("f_scale", [P, K])
        br = sb("br", [P, 10, BRANCHES])
        w_diag = sb("w_diag", [P, BRANCHES, 2, P])
        mu_raw = sb("mu_raw", [P, BRANCHES, 3 * C])
        mu = sb("mu", [P, 4, 3, C])
        ring = sb("ring", [P, NSLOT * 2 * HLEN])
        ring_h = ring[:].bitcast(F16).rearrange("s (n p h c) -> s n p h c", n=NSLOT, p=2, h=2)
        ring_m = sb("ring_m", [P, NSLOT, 2 * 3 * C])
        u_conv = sb("u_conv", [P, 2, 2, 2, P])
        o_sb = sb("o_sb", [P, 2, 2 * P])
        m_raw = ring[:, 0:BRANCHES * 2 * 8 * C].rearrange("d (r m k e) -> d r m k e", r=BRANCHES, m=2, k=8)
        m_size = 8 * 3 * C
        m_out = [a[:, 0:m_size].rearrange("d (k p e) -> d k p e", k=8, p=3) for a in (
            x_both, x_both[:, m_size:], n_tok[:].rearrange("s q p b c -> s (q p b c)"), n_pad[:].rearrange("c b y x -> c (b y x)"))]

        bank = [ctx.enter_context(nc.psum_tensor(f"bank{i}", [P, 512], F32)) for i in range(8)]
        conv_ps, acc_ps = bank[0:2], bank[2:4]
        val_ps, tail_ps, off_ps, tok_ps = bank[4:6], bank[6], bank[7], bank[7]
        y_ps, y_chan_ps = tail_ps[:, 256:256 + 2 * C], tail_ps[:, 384:384 + P]

        s_x = [sem(f"s_x{i}") for i in range(BP)]
        s_ident, s_const, s_woff, s_w, s_bn, s_phi, s_mats, s_small = (
            sem(n) for n in ("s_ident", "s_const", "s_woff", "s_w", "s_bn", "s_phi", "s_mats", "s_small"))
        ones_ready = sem("ones_ready")
        zeroed, border_stored, padded_stored = sem("zeroed"), sem("border_stored"), [sem(f"padded_stored{i}") for i in range(BP)]
        table_stored = [sem(f"table_stored{i}") for i in range(BP)]
        x_reversed = sem("x_reversed")
        x_turned, x_copied, n_ready, n_turned, n_copied = (
            sem(n) for n in ("x_turned", "x_copied", "n_ready", "n_turned", "n_copied"))
        woff_ready, woff_turned, woff_copied = sem("woff_ready"), sem("woff_turned"), sem("woff_copied")
        w_ready, w_turned, w_copied = sem("w_ready"), sem("w_turned"), sem("w_copied")
        phi_turned, f_rows_ready, f_rows_stored = sem("phi_turned"), sem("f_rows_ready"), sem("f_rows_stored")
        diag_ready, f_scale_ready, f_scale_done = sem("diag_ready"), sem("f_scale_ready"), sem("f_scale_done")
        w_diag_ready, mats_summed = sem("w_diag_ready"), sem("mats_summed")
        mats_ready, mats_stored, mu_ready = sem("mats_ready"), sem("mats_stored"), sem("mu_ready")
        off_done, off_laid, off_turned, off_copied, mask_exp = (
            sem(n) for n in ("off_done", "off_laid", "off_turned", "off_copied", "mask_exp"))
        br_ready, br_exp = sem("br_ready"), sem("br_exp")
        idx_ready = sem("idx_ready")
        gathered = [sem(f"gathered{i}") for i in range(BLK)]
        v_ready = [sem(f"v_ready{i}") for i in range(2)]
        val_copied, y_done, y_exp, y_used, u_ready = (
            sem(n) for n in ("val_copied", "y_done", "y_exp", "y_used", "u_ready"))
        val_turned, y_convolved, y_copied = sem("val_turned"), sem("y_convolved"), sem("y_copied")
        u_turned, u_copied = sem("u_turned"), sem("u_copied")
        filt_loaded = [sem(f"filt_loaded{i}") for i in range(NSLOT)]
        filt_used = [sem(f"filt_used{i}") for i in range(NSLOT)]
        conv_done = [sem(f"conv_done{i}") for i in range(2)]
        conv_copied = [sem(f"conv_copied{i}") for i in range(2)]
        out_copied, out_stored = sem("out_copied"), [sem(f"out_stored{i}") for i in range(2)]
        dve_step = sem("dve_step")

        pool_marks, pe_marks, dve_marks, act_marks = (sem(f"{n}_marks") for n in ("pool", "pe", "dve", "act"))

        N_SMALL = 3
        block = ctx.enter_context(nc.Block())

        @block.sync
        def _(sp):
            sp.dma_start(ident_swap[:], ident_in).then_inc(s_ident, 16)
            for bp in range(BP):
                sp.dma_start(x_ch[:, bp, :], ap(x, bp * 2 * C * T, [[T, P], [1, T]])).then_inc(s_x[bp], 16)
            sp.dma_start(w_off_raw[0:2 * TAPS, :], ap(offset_w, 0, [[C * TAPS, 2 * TAPS], [1, C * TAPS]])).then_inc(s_woff, 16)
            sp.dma_start(w_off_raw[2 * TAPS:NOFF, :], ap(mask_w, 0, [[C * TAPS, TAPS], [1, C * TAPS]])).then_inc(s_woff, 16)
            sp.dma_start(grid[:], grid_in).then_inc(s_const, 16)
            sp.dma_start(first_row[:], first_row_in).then_inc(s_const, 16)
            sp.dma_start(off_bias[:, 0:2 * TAPS], ap(offset_b, 0, [[0, P], [1, 2 * TAPS]])).then_inc(s_const, 16)
            sp.dma_start(off_bias[:, 2 * TAPS:NOFF], ap(mask_b, 0, [[0, P], [1, TAPS]])).then_inc(s_const, 16)
            sp.dma_start(sig[:, 0, :], ap(sigma, 0, [[0, P], [1, K]])).then_inc(s_small, 16)
            sp.dma_start(br[:, 0, :], ap(log_weights, 0, [[0, P], [1, BRANCHES]])).then_inc(s_small, 16)
            sp.dma_start(br[:, 1, :], ap(gumbel, 0, [[0, P], [1, BRANCHES]])).then_inc(s_small, 16)
            sp.wait_ge(zeroed, 1)
            edge = PW * C
            for b in range(B):
                for r in (0, PH - 1):
                    sp.dma_start(ap(padded, (b * PH + r) * edge, [[edge // 16, 16], [1, edge // 16]]),
                                 zeros[0:16, :]).then_inc(border_stored, 16)
            for col in (0, PW - 1):
                sp.dma_start(ap(padded, edge + col * C, [[PH * edge, B], [edge, H], [1, C]]),
                             zeros[:, 0:C]).then_inc(border_stored, 16)
            sp.dma_start(phi_sb[:], ap(phi, 0, [[2 * K, P], [2 * P * K, NJ], [1, 2 * K]])).then_inc(s_phi, 16)
            sp.wait_ge(border_stored, 16 * (2 * B + 2))

            def store_table(bp):
                sp.wait_ge(n_ready, bp + 1)
                for j in range(NJ):
                    for b2 in range(2):
                        b = 2 * bp + b2
                        dst = ap(padded, ((b * PH + 1 + H - 8 * (j + 1)) * PW + 1) * C, [[edge, 8], [2 * C, 16], [1, 2 * C]])
                        sp.dma_start(dst, n_store[:, 4 * bp + j, b2, :, :]).then_inc(padded_stored[bp], 16)
                sp.wait_ge(padded_stored[bp], 16 * 2 * NJ)
                for b2 in range(2):
                    for cy in range(2):
                        sp.dma_start(ap(table[bp], b2 * SIDE * SIDE * ROW + cy * 2 * C, [[SIDE * ROW, SIDE], [ROW, SIDE], [1, 2 * C]]),
                                     ap(padded, ((2 * bp + b2) * PH + cy) * edge, [[edge, SIDE], [C, SIDE], [1, 2 * C]])
                                     ).then_inc(table_stored[bp], 16)

            def load_matrices():
                for i, m in enumerate((m_plus, m_minus)):
                    for kh in range(2):
                        for r in range(BRANCHES):
                            sp.dma_start(m_raw[C * kh:C * kh + C, r, i, :, :],
                                          ap(m, (r * K + 8 * kh) * C * C, [[C, C], [C * C, 8], [1, C]])).then_inc(s_mats, 16)
                for half in range(2):
                    for r in range(BRANCHES):
                        sp.dma_start(mu_raw[C * half:C * half + C, r, :],
                                      ap(m_u, r * 3 * C * C, [[C, C], [C * C, 3], [1, C]])).then_inc(s_mats, 16)

            store_table(0)
            load_matrices()
            sp.wait_ge(f_rows_ready, 1)
            sp.dma_start(ap(hankel, 0, [[4 * HROW, K], [1, 4 * HROW]]), f_rows[:].rearrange("k p h c -> k (p h c)")
                         ).then_inc(f_rows_stored, 16)
            for r in range(BRANCHES):
                sp.wait_ge(mats_ready, 2 * (r + 1))
                for kh in range(2):
                    sp.dma_start(ap(mix_d, 8 * kh * C * 12 * C + (3 - r) * 3 * C, [[12 * C, C], [C * 12 * C, 8], [1, 3 * C]]),
                                 m_out[r][C * kh:C * kh + C].rearrange("d k p e -> d k (p e)")).then_inc(mats_stored, 16)
            store_table(1)
            sp.wait_ge(f_rows_stored, 16)
            sp.wait_ge(mats_stored, 32 * BRANCHES)
            for n in range(NQ):
                ncol = 2 + P * (n % NJ + 1)
                seg0, nseg = unit_ranges(n % NJ)
                with sp.Fori(0, 2) as i:
                    for kk in range(8):
                        slot = kk % NSLOT
                        sp.wait_ge(filt_used[slot], START + 4 * n + 2 * i + kk // NSLOT)
                        k = 8 * i + kk
                        sp.dma_start(ring_h[:, slot].rearrange("s p h c -> s (p h) c")[:, :, 0:ncol],
                                     ap(hankel, k * 4 * HROW + HPAD - 2 - (P - 1), [[1, P], [HROW, 4], [1, ncol]])
                                     ).then_inc(filt_loaded[slot], 16)
                        sp.dma_start(ring_m[:, slot, 0:(3 * nseg - 1) * C],
                                     ap(mix_d, k * C * 12 * C + seg0 * 3 * C, [[C, 2], [12 * C, C], [1, (3 * nseg - 1) * C]])
                                     ).then_inc(filt_loaded[slot], 16)

        @block.gpsimd
        def _(pool):
            pool.memset(zeros[:], 0.0).then_inc(zeroed, 1)
            pool.memset(n_pad[:], 0.0)
            pool.memset(w_off[:], 0.0).then_inc(zeroed, 1)
            pool.memset(uT[:, :, :, 0:1], 0.0).then_inc(zeroed, 1)
            for bp in range(BP):
                pool.wait_ge(table_stored[bp], 16 * 4)
                with pool.Fori(0, NJ // 2) as i:
                    for h in range(2):
                        q = 4 * bp + 2 * i + h
                        pool.wait_ge(idx_ready, q + 1)
                        for k in range(BLK):
                            pool.wait_ge(v_ready[k % 2], START + 2 * q + k // 2 - 1)
                            pool.sem_inc(pool_marks, 1)
                            for tap in range(TAPS):
                                pool.indirect_dma_start(
                                    G[:, k, tap, :], None, table[bp],
                                    bass.IndirectOffsetOnAxis(ap=idx[:, h, k, tap:tap + 1], axis=0)
                                ).then_inc(gathered[k], 16)

        @block.vector
        def _(dve):
            steps = [0]

            def chain(ins):
                steps[0] += 1
                ins.then_inc(dve_step, 1)
                dve.wait_ge(dve_step, steps[0])

            def rsqrt(y, v, t):
                link(dve.tensor_scalar(t.bitcast(I32), v.bitcast(I32), 1, None, ALU.logical_shift_right))
                link(dve.tensor_scalar(y.bitcast(I32), t.bitcast(I32), -1.0, RSQRT_SEED, ALU.mult, ALU.add))
                for _ in range(3):
                    link(dve.scalar_tensor_tensor(t, y, -0.5, y, ALU.mult, ALU.mult))
                    link(dve.tensor_tensor(t, t, v, ALU.mult))
                    link(dve.scalar_tensor_tensor(y, t, 1.5, y, ALU.add, ALU.mult))

            link = chain

            for s in (*v_ready, y_used):
                dve.sem_inc(s, START)
            dve.memset(ones[:], 1.0).then_inc(ones_ready, 1)
            dve.memset(vT[C:C + 1, :, 4, :], 1.0)
            dve.memset(f_rows[:], 0.0)
            for bp in range(BP):
                dve.wait_ge(s_x[bp], 16)
                dve.tensor_copy(x_rev[:, bp, :], x_ch[:, bp, ::-1]).then_inc(x_reversed, 1)
            dve.wait_ge(s_woff, 32)
            raw = w_off_raw[:].rearrange("o (c t) -> o t c", t=TAPS)
            dve.tensor_copy(w_off_dup[:, :, 0, :], raw)
            dve.tensor_copy(w_off_dup[:, :, 1, :], raw).then_inc(woff_ready, 1)
            dve.wait_ge(s_const, 64)
            link(dve.tensor_tensor(grid[:], grid[:], off_bias[:].unsqueeze(1).broadcast_to([P, 8, NOFF]), ALU.subtract))
            for bp in range(BP):
                qs = slice(4 * bp, 4 * bp + 4)
                xs = x_tok[:, qs].rearrange("s q p b c -> s (q p b) c")
                ns = n_tok[:, qs].rearrange("s q p b c -> s (q p b) c")
                tmp = G[:, 2 * bp, 0:4, :].rearrange("s t r -> s (t r)").rearrange("s (g c) -> s g c", c=C)
                dve.wait_ge(x_copied, 2 * (bp + 1))
                link(dve.tensor_reduce(stat[:, 0, :], xs, AX.X, ALU.add))
                link(dve.tensor_scalar(stat[:, 1, :], stat[:, 0, :], 1.0 / C, None, ALU.mult))
                link(dve.tensor_tensor(ns, xs, stat[:, 1, :].unsqueeze(2).broadcast_to([P, 16, C]), ALU.subtract))
                link(dve.tensor_tensor(tmp, ns, ns, ALU.mult))
                link(dve.tensor_reduce(stat[:, 2, :], tmp, AX.X, ALU.add))
                link(dve.tensor_scalar(stat[:, 3, :], stat[:, 2, :], 1.0 / C, LN1_EPS, ALU.mult, ALU.add))
                rsqrt(stat[:, 4, :], stat[:, 3, :], stat[:, 5, :])
                link(dve.tensor_tensor(ns, ns, stat[:, 4, :].unsqueeze(2).broadcast_to([P, 16, C]), ALU.mult))
                for p in range(2):
                    last = dve.tensor_copy(n_store[:, qs, :, 1 - p, :], n_tok[:, qs, p])
                last.then_inc(n_ready, 1)

            def offsets(bp):
                dve.wait_ge(off_turned, bp + 1)
                for b2 in range(2):
                    dst = offs[:, 4 * bp:4 * bp + 4, b2::2, :].rearrange("s (g j) p n -> s g (j p) n", g=2)
                    src = off_ps[:, 256 * b2:256 * b2 + 256].rearrange("s (m g n) -> s g m n", m=4, g=2)
                    last = dve.tensor_tensor(dst, grid[:].rearrange("s (g m) n -> s g m n", g=2), src[:, :, :, 0:NOFF], ALU.subtract)
                last.then_inc(off_copied, 1)
                dve.wait_ge(off_copied, bp + 1)

            def masks(bp):
                m = mask[:, 4 * bp:4 * bp + 4].rearrange("s q k t -> s (q k t)")
                dve.wait_ge(mask_exp, bp + 1)
                link(dve.tensor_scalar(m, m, 1.0, None, ALU.add))
                link(dve.reciprocal(m, m))

            def positions(q, slot, masks=None):
                o = offs[:, q] if isinstance(q, int) else offs[:, bass.ds(q, 1)].rearrange("s o k n -> s (o k) n")
                mk = mask[:, q] if isinstance(q, int) else mask[:, bass.ds(q, 1)].rearrange("s o k n -> s (o k) n")
                pk = pos[:].rearrange("s k t a -> s k (t a)")
                link(dve.tensor_scalar(pk, o[:, :, 0:2 * TAPS], 0.0, float(H + 1), ALU.max, ALU.min))
                link(dve.tensor_copy(pos_i[:], pos[:]))
                link(dve.tensor_tensor(corner[:], pos_i[:], pos[:], ALU.is_gt))
                link(dve.tensor_tensor(corner[:], pos_i[:], corner[:], ALU.subtract))
                link(dve.tensor_scalar(corner[:], corner[:], float(H), None, ALU.min))
                dve.tensor_tensor(frac[:], pos[:], corner[:], ALU.subtract)
                link(dve.scalar_tensor_tensor(idx_f[:], corner[:, :, :, 0], float(SIDE), corner[:, :, :, 1], ALU.mult, ALU.add))
                dve.tensor_tensor(idx[:, slot], idx_f[:], first_row[:].unsqueeze(2).broadcast_to([P, BLK, TAPS]), ALU.add
                                  ).then_inc(idx_ready, 1)
                if masks:
                    masks()
                link(dve.tensor_scalar(anti[:], frac[:], -1.0, 1.0, ALU.mult, ALU.add))
                dve.tensor_tensor(my[:, 0], mk, anti[:, :, :, 0], ALU.mult)
                link(dve.tensor_tensor(my[:, 1], mk, frac[:, :, :, 0], ALU.mult))
                for cy in range(2):
                    dve.tensor_tensor(wts[:, slot, :, :, 2 * cy], my[:, cy], anti[:, :, :, 1], ALU.mult)
                    last = dve.tensor_tensor(wts[:, slot, :, :, 2 * cy + 1], my[:, cy], frac[:, :, :, 1], ALU.mult)
                link(last)

            dve.wait_ge(s_small, 16 * N_SMALL)
            link(dve.tensor_tensor(br[:, 2, :], br[:, 0, :], br[:, 1, :], ALU.add))
            link(dve.tensor_reduce(br[:, 3, 0:1], br[:, 2, :], AX.X, ALU.max))
            dve.tensor_scalar(br[:, 4, :], br[:, 2, :], br[:, 3, 0:1], None, ALU.subtract).then_inc(br_ready, 1)
            for r in range(BRANCHES):
                dve.memset(br[:, 8, r:r + 1], float(BRANCHES - r))
            rsqrt(sig[:, 1, :], sig[:, 0, :], sig[:, 2, :])
            link(dve.tensor_tensor(sig[:, 1, :], sig[:, 1, :], sig[:, 0, :], ALU.mult))
            rsqrt(sig[:, 3, :], sig[:, 1, :], sig[:, 2, :])
            link(dve.tensor_tensor(sig[:, 3, :], sig[:, 3, :], sig[:, 1, :], ALU.mult))
            offsets(0)
            positions(0, 0, lambda: masks(0))
            dve.wait_ge(br_exp, 1)
            link(dve.reciprocal(br[:, 3, 2:3], br[:, 3, 1:2]))
            link(dve.tensor_scalar(br[:, 6, :], br[:, 5, :], br[:, 3, 2:3], None, ALU.mult))
            link(dve.tensor_reduce(br[:, 3, 3:4], br[:, 6, :], AX.X, ALU.max))
            link(dve.scalar_tensor_tensor(br[:, 7, :], br[:, 6, :], br[:, 3, 3:4], br[:, 8, :], ALU.is_ge, ALU.mult))
            link(dve.tensor_reduce(br[:, 3, 0:1], br[:, 7, :], AX.X, ALU.max))
            link(dve.tensor_scalar(br[:, 7, :], br[:, 7, :], br[:, 3, 0:1], None, ALU.is_equal))
            link(dve.tensor_tensor(br[:, 7, :], br[:, 7, :], br[:, 6, :], ALU.subtract))
            link(dve.tensor_tensor(br[:, 9, :], br[:, 7, :], br[:, 6, :], ALU.add))
            for r in range(BRANCHES):
                for sign in range(2):
                    last = dve.tensor_scalar(w_diag[:, r, sign, :], ident, br[:, 9, r:r + 1], 1.0 - 2.0 * sign, ALU.mult, ALU.mult)
            last.then_inc(w_diag_ready, 1)
            dve.wait_ge(s_bn, 16 * 6)
            bn = bn_row[C:C + 1]
            tmp = expo[C:C + 1]
            link(dve.tensor_scalar(bn[:, 3, :], bn[:, 3, :], BN_EPS, None, ALU.add))
            rsqrt(tmp[:, 0, :], bn[:, 3, :], tmp[:, 1, :])
            link(dve.tensor_tensor(bn[:, 0, :], bn[:, 0, :], tmp[:, 0, :], ALU.mult))
            link(dve.tensor_tensor(bn[:, 2, :], bn[:, 2, :], bn[:, 0, :], ALU.mult))
            dve.tensor_tensor(w_main[C:C + 1, 4, :], bn[:, 1, :], bn[:, 2, :], ALU.subtract).then_inc(w_ready, 1)
            dve.wait_ge(s_w, 16)
            link(dve.tensor_scalar(bn_col[:, 1:2], bn_col[:, 1:2], BN_EPS, None, ALU.add))
            rsqrt(st2[0:C, 0, 0:1], bn_col[:, 1:2], st2[0:C, 1, 0:1])
            link(dve.tensor_tensor(bn_col[:, 0:1], bn_col[:, 0:1], st2[0:C, 0, 0:1], ALU.mult))
            dve.tensor_scalar(w_scaled[:].rearrange("o (t c) -> o t c", t=TAPS),
                              w_raw[:].rearrange("o (c t) -> o t c", t=TAPS), bn_col[:, 0:1], None, ALU.mult
                              ).then_inc(w_ready, 1)

            dve.wait_ge(phi_turned, 1)
            for par in range(2):
                last = dve.tensor_reduce(f_max[:, 2 + par:3 + par], val_ps[par][0:K, :], AX.X, ALU.max, apply_absolute_value=True)
            link(last)
            link(dve.tensor_tensor(f_max[:, 0:1], f_max[:, 2:3], f_max[:, 3:4], ALU.max))
            link(dve.tensor_scalar(f_max[:, 0:1], f_max[:, 0:1], 1e-30, 1.0 / PHI_SCALE, ALU.max, ALU.mult))
            link(dve.reciprocal(f_max[:, 1:2], f_max[:, 0:1]))
            for par in range(2):
                row = f_rows[:, par, :, HPAD:HPAD + HALF]
                link(dve.tensor_scalar(row[:, 0, :], val_ps[par][0:K, :], f_max[:, 1:2], None, ALU.mult))
                last = dve.scalar_tensor_tensor(row[:, 1, :], val_ps[par][0:K, :], f_max[:, 1:2], row[:, 0, :], ALU.mult, ALU.subtract)
            last.then_inc(f_rows_ready, 1)
            link(dve.reciprocal(f_max[:, 2:3], f_max[:, 1:2]))
            dve.tensor_scalar(f_diag[:], ident[0:K, 0:K], f_max[:, 2:3], None, ALU.mult).then_inc(diag_ready, 1)


            def weigh(q, slot, p, b2):
                k = 2 * p + b2
                dve.wait_ge(gathered[k], 16 * TAPS * (q + 1))
                g = G[:, k].rearrange("s t (n c) -> s (t n) c", c=C)
                w = wts[:, slot, k].rearrange("s t n -> s (t n)").unsqueeze(2).broadcast_to([P, 4 * TAPS, C])
                link(dve.tensor_tensor(g, g, w, ALU.mult))
                link(dve.tensor_tensor(G[:, k, :, 0:2 * C], G[:, k, :, 0:2 * C], G[:, k, :, 2 * C:4 * C], ALU.add))
                if b2 == 0:
                    dve.wait_ge(val_turned, START + 2 * q + p)
                dve.tensor_tensor(V[:, b2].rearrange("s (t c) -> s t c", c=C), G[:, k, :, 0:C], G[:, k, :, C:2 * C], ALU.add
                                  ).then_inc(v_ready[b2], 1)

            def activate(q, p):
                r = 2 * q + p
                xs = x_tok[:, bass.ds(q, 1), p].rearrange("s o b c -> s (o b) c")
                x2 = x2_tok[:, bass.ds(r, 1)].rearrange("s o b c -> s (o b) c")
                dve.wait_ge(y_exp, r + 1)
                link(dve.tensor_scalar(expo[:], expo[:], 1.0, None, ALU.add))
                link(dve.reciprocal(sil[:], expo[:]))
                dve.tensor_tensor(sil[:], y_ps.rearrange("s (b c) -> s b c", b=2), sil[:], ALU.mult).then_inc(y_used, 1)
                dve.wait_ge(y_used, START + r + 1)
                link(dve.tensor_tensor(x2, xs, sil[:], ALU.add))
                dve.sem_inc(dve_marks, 1)

            def normalise(q, p):
                r = 2 * q + p
                x2 = x2_tok[:, bass.ds(r, 1)].rearrange("s o b c -> s (o b) c")
                hi = u_hi[:, bass.ds(q, 1), :, p].rearrange("s o b c -> s (o b) c")
                lo = u_lo[:, bass.ds(q, 1), :, p].rearrange("s o b c -> s (o b) c")
                u = u_tok[:].rearrange("s (b c) -> s b c", b=2)
                link(dve.tensor_reduce(st2[:, 0, :], x2, AX.X, ALU.add))
                link(dve.tensor_scalar(st2[:, 1, :], st2[:, 0, :], 1.0 / C, None, ALU.mult))
                link(dve.tensor_tensor(cen[:], x2, st2[:, 1, :].unsqueeze(2).broadcast_to([P, 2, C]), ALU.subtract))
                link(dve.tensor_tensor(sq[:], cen[:], cen[:], ALU.mult))
                link(dve.tensor_reduce(st2[:, 2, :], sq[:], AX.X, ALU.add))
                link(dve.tensor_scalar(st2[:, 3, :], st2[:, 2, :], 1.0 / C, LN2_EPS, ALU.mult, ALU.add))
                rsqrt(st2[:, 4, :], st2[:, 3, :], st2[:, 5, :])
                dve.wait_ge(u_turned, START + r)
                link(dve.tensor_tensor(u, cen[:],
                                       st2[:, 4, :].unsqueeze(2).broadcast_to([P, 2, C]), ALU.mult))
                link(dve.tensor_scalar(hi, u, U_SCALE, None, ALU.mult))
                dve.scalar_tensor_tensor(lo, u, U_SCALE, hi, ALU.mult, ALU.subtract).then_inc(u_ready, 1)

            def finish(q, p):
                activate(q, p)
                normalise(q, p)

            def quarter(q, slot):
                positions(q + 1, 1 - slot)
                weigh(q, slot, 1, 0)
                finish(q, 0)
                weigh(q, slot, 1, 1)
                weigh(q + 1, 1 - slot, 0, 0)
                finish(q, 1)
                weigh(q + 1, 1 - slot, 0, 1)

            weigh(0, 0, 0, 0)
            offsets(1)
            positions(1, 1)
            weigh(0, 0, 0, 1)
            weigh(0, 0, 1, 0)
            dve.wait_ge(f_scale_ready, 1)
            dve.scalar_tensor_tensor(f_scale[:], bank[3][:, 0:K], 1.0 / U_SCALE, sig[:, 3, :], ALU.mult, ALU.mult
                                     ).then_inc(f_scale_done, 1)
            activate(0, 0)
            weigh(0, 0, 1, 1)
            normalise(0, 0)
            finish(0, 1)
            masks(1)
            weigh(1, 1, 0, 0)
            weigh(1, 1, 0, 1)
            per_loop = LINKS_PER_QUARTER * 2
            with dve.Fori(0, NQ // 2 - 1) as i:
                at0 = steps[0]

                def link(ins, i=i, at0=at0):
                    steps[0] += 1
                    ins.then_inc(dve_step, 1)
                    dve.wait_ge(dve_step, steps[0] + per_loop * i)
                quarter(2 * i + 1, 1)
                quarter(2 * i + 2, 0)
                assert steps[0] - at0 == per_loop, (steps[0] - at0)
            steps[0] += per_loop * (NQ // 2 - 2)
            link = chain
            weigh(NQ - 1, 1, 1, 0)
            finish(NQ - 1, 0)
            weigh(NQ - 1, 1, 1, 1)
            finish(NQ - 1, 1)

        @block.scalar
        def _(act):
            act.dma_start(w_raw[:], ap(weight, 0, [[C * TAPS, C], [1, C * TAPS]])).then_inc(s_w, 16)
            for i, v in enumerate((gamma, var)):
                act.dma_start(bn_col[:, i:i + 1], ap(v, 0, [[1, C], [1, 1]])).then_inc(s_bn, 16)
            for i, v in enumerate((gamma, beta, mean, var)):
                act.dma_start(bn_row[C:C + 1, i, :], ap(v, 0, [[C, 1], [1, C]])).then_inc(s_bn, 16)
            for s in (u_copied, *conv_copied):
                act.sem_inc(s, START)
            act.wait_ge(ones_ready, 1)
            act.activation(f_max[:, 0:1], ones[:, 0:1], ACT.Exp)
            for g in range(4):
                bp, jj = divmod(g, 2)
                act.wait_ge(x_turned, g + 1)
                act.copy(x_tok[:, 4 * bp + 2 * jj:4 * bp + 2 * jj + 2].rearrange("s q p b c -> s (q p b c)"),
                         bank[g][:]).then_inc(x_copied, 1)
            act.wait_ge(woff_turned, 1)
            act.wait_ge(zeroed, 2)
            act.copy(w_off[:, :, 0:NOFF], bank[6][:, 0:TAPS * NOFF].rearrange("c (t n) -> c t n", t=TAPS)).then_inc(woff_copied, 1)

            def lay_out_normalised(bp):
                for jj in range(2):
                    act.wait_ge(n_turned, 2 * bp + jj + 1)
                    for p in range(2):
                        last = act.copy(n_pad[:, bp, 17 - 16 * jj:33 - 16 * jj, 2 - p:2 - p + W - 1:2],
                                        bank[2 + jj][:, 256 * p:256 * p + 256].rearrange("c (y x) -> c y x", x=16))
                    last.then_inc(n_copied, 1)

            def lay_out_offsets(bp):
                act.wait_ge(off_done, bp + 1)
                if bp:
                    act.wait_ge(off_turned, bp)
                act.copy(off_ch[:, 0, :], bank[0][:])
                act.copy(off_ch[:, 1, :], bank[1][:]).then_inc(off_laid, 1)

            def exp_masks(bp):
                act.wait_ge(off_copied, bp + 1)
                qs = slice(4 * bp, 4 * bp + 4)
                act.activation(mask[:, qs].rearrange("s q k t -> s (q k) t"),
                               offs[:, qs].rearrange("s q k n -> s (q k) n")[:, :, 2 * TAPS:NOFF], ACT.Exp).then_inc(mask_exp, 1)

            lay_out_normalised(0)
            act.wait_ge(br_ready, 1)
            act.activation(br[:, 5, :], br[:, 4, :], ACT.Exp, accum_out=br[:, 3, 1:2]).then_inc(br_exp, 1)
            lay_out_offsets(0)
            exp_masks(0)
            lay_out_normalised(1)
            lay_out_offsets(1)
            act.wait_ge(w_turned, 1)
            act.copy(w_main[:, 0:4, :], bank[6][:, 0:4 * C].rearrange("k (t o) -> k t o", t=4))
            act.copy(w_main[0:C, 4, :], bank[6][0:C, 4 * C:5 * C]).then_inc(w_copied, 1)
            for r in range(BRANCHES):
                for par in range(2):
                    act.wait_ge(mats_summed, 3 * r + par + 1)
                    sums = bank[par][:].rearrange("d (k e) -> d k e", k=8)
                    if par == 0:
                        act.copy(m_out[r][:, :, 2, :], sums)
                    act.copy(m_out[r][:, :, par, :], sums).then_inc(mats_ready, 1)
                act.wait_ge(mats_summed, 3 * r + 3)
                act.copy(mu[:, 3 - r].rearrange("d i e -> d (i e)"), bank[2][:, 0:3 * C]).then_inc(mu_ready, 1)

            def copy_values(r):
                act.wait_ge(val_turned, START + r + 1)
                for b2 in range(2):
                    act.copy(vT[:, b2, 0:4, :], val_ps[b2][:].rearrange("k (m s) -> k m s", m=4))
                act.copy(vT[0:C, :, 4, :], tail_ps[0:C, 0:256].rearrange("k (b s) -> k b s", b=2)).then_inc(val_copied, 1)

            def copy_convolved(r):
                act.wait_ge(y_convolved, r + 1)
                act.copy(y_chan[:], y_chan_ps).then_inc(y_copied, 1)

            def exp_y(r):
                act.wait_ge(y_done, r + 1)
                act.wait_ge(y_used, START + r)
                act.activation(expo[:], y_ps.rearrange("s (b c) -> s b c", b=2), ACT.Exp, scale=-1.0).then_inc(y_exp, 1)

            def copy_tokens(q, i):
                act.wait_ge(u_turned, START + 2 * q + i + 1)
                act.copy(uT[:, bass.ds(i, 1), q // NJ, 1 + P * (q % NJ):1 + P * (q % NJ) + P].rearrange("c o a -> c (o a)"),
                         tok_ps[:, 0:P]).then_inc(u_copied, 1)

            copy_values(0)
            copy_convolved(0)
            exp_y(0)
            copy_values(1)
            copy_convolved(1)
            exp_y(1)
            exp_masks(1)
            copy_tokens(0, 0)
            copy_tokens(0, 1)
            act.wait_ge(f_scale_done, 1)

            def copy_products(n, kk, i):
                k = bass.ds(8 * i + kk, 1)
                for b2 in range(2):
                    act.wait_ge(conv_done[b2], 16 * n + 8 * i + kk + 1)
                    act.sem_inc(act_marks, 1)
                    if n % NJ == 0:
                        last = act.activation(u_conv[:, kk % 2, b2], conv_ps[b2][:, 0:2 * P].rearrange("c (p a) -> c p a", p=2),
                                              ACT.Copy, scale=f_scale[:, k])
                    else:
                        for src, (first, stride) in enumerate(((1, NCOL), (NCOL, 1 - NCOL))):
                            half = slice(C * src, C * src + C)
                            c = conv_ps[b2][half, :]
                            c = bass.AP(c.tensor, c.offset + first, [c.ap[0], [stride, 2], [1, P]])
                            last = act.activation(u_conv[half, kk % 2, b2], c, ACT.Copy, scale=f_scale[half, k])
                    last.then_inc(conv_copied[b2], 1)

            for n in range(NQ):
                with act.Fori(0, 2) as i:
                    r = 2 * n + 2 + i
                    for kk in range(8):
                        copy_products(n, kk, i)
                        if n + 1 < NQ and kk == VALUES_AT:
                            copy_values(r)
                        if n + 1 < NQ and kk == Y_AT:
                            copy_convolved(r)
                        if n + 1 < NQ and kk == Y_TURN_AT:
                            exp_y(r)
                        if n + 1 < NQ and kk == TOKENS_AT:
                            copy_tokens(n + 1, i)
                act.wait_ge(filt_used[NSLOT - 1], START + 4 * (n + 1))
                if n >= 2:
                    act.wait_ge(out_stored[n % 2], 16 * (n // 2))
                act.copy(o_sb[:, n % 2, :].rearrange("e (a p) -> e p a", p=2),
                         acc_ps[n % 2][:, 0:2 * P].rearrange("e (p a) -> e p a", p=2)).then_inc(out_copied, 1)
                act.wait_ge(out_copied, n + 1)
                act.dma_start(ap(out, (n // NJ) * 2 * C * T + 2 * P * (n % NJ), [[T, P], [1, 2 * P]]),
                              o_sb[:, n % 2, :]).then_inc(out_stored[n % 2], 16)
            for stored in out_stored:
                act.wait_ge(stored, 16 * NQ // 2)

        @block.tensor
        def _(pe):
            for s in (val_turned, u_turned, *filt_used):
                pe.sem_inc(s, START)
            pe.wait_ge(s_ident, 16)
            for g in range(4):
                bp, jj = divmod(g, 2)
                if jj == 0:
                    pe.wait_ge(x_reversed, bp + 1)
                for j2 in range(2):
                    for p in range(2):
                        t = T - 255 - 256 * (2 * jj + j2) - p
                        last = pe.transpose(bank[g][:, P * (2 * j2 + p):P * (2 * j2 + p) + P], x_rev[:, bp, t:t + 255:2], ident)
                last.then_inc(x_turned, 1)
            pe.wait_ge(woff_ready, 1)
            for t in range(TAPS):
                last = pe.transpose(bank[6][:, NOFF * t:NOFF * t + NOFF], w_off_dup[:, t].rearrange("o h c -> o (h c)"),
                                    ident[0:NOFF, 0:NOFF])
            last.then_inc(woff_turned, 1)

            def keep_warm(n, idle_bank):
                for _ in range(n):
                    pe.matmul(idle_bank[:], ident, x_rev[:, BP - 1, T - 512:T], start=True, stop=True)

            def turn_normalised(bp):
                pe.wait_ge(n_ready, bp + 1)
                pe.wait_ge(x_copied, 4)
                for jj in range(2):
                    for j2 in range(2):
                        for p in range(2):
                            last = pe.transpose(bank[2 + jj][:, 256 * p + P * (1 - j2):256 * p + P * (1 - j2) + P],
                                                n_tok[:, 4 * bp + 2 * jj + j2, p].rearrange("s b c -> s (b c)"), ident)
                    last.then_inc(n_turned, 1)

            def convolve_offsets(bp):
                pe.wait_ge(n_copied, 2 * (bp + 1))
                if bp:
                    pe.wait_ge(off_laid, bp)
                pe.wait_ge(woff_copied, 1)
                for t in range(len(TAP_HALVES[0])):
                    for b2 in range(2):
                        for tg in range(2):
                            if t == len(TAP_HALVES[tg]):
                                continue
                            tap = TAP_HALVES[tg][t]
                            dy, dx = divmod(tap, 3)
                            for jj in range(2):
                                half = slice(C * b2, C * b2 + C)
                                y0, x0 = 18 - 16 * jj - dy, 2 - dx
                                a = n_pad[half, bp, y0:y0 + 16, x0:x0 + W - 1:2]
                                a = bass.AP(a.tensor, a.offset, [a.ap[0], [1, 2], *a.ap[1:]])
                                group = NCH * (2 * tg + jj)
                                last = pe.matmul(bank[b2][group:group + NCH, :], w_off[half, tap, :], a,
                                                 start=(t == 0), stop=(tap == TAP_HALVES[tg][-1]))
                last.then_inc(off_done, 1)

            def turn_offsets(bp):
                pe.wait_ge(off_laid, bp + 1)
                if bp:
                    pe.wait_ge(off_copied, bp)
                for b2 in range(2):
                    for j2 in range(2):
                        for p in range(2):
                            col = 64 * (4 * b2 + 2 * j2 + p)
                            src = 256 * (1 - p) + P * (1 - j2)
                            last = pe.matmul(off_ps[:, col:col + 64], off_ch[:, b2, src:src + P], fold, start=True, stop=True)
                last.then_inc(off_turned, 1)

            pe.wait_ge(woff_copied, 1)
            keep_warm(WARM_UP, bank[6])
            turn_normalised(0)
            keep_warm(1, bank[6])
            convolve_offsets(0)
            turn_offsets(0)
            turn_normalised(1)
            pe.wait_ge(s_phi, 16)
            for par in range(2):
                for j in range(NJ):
                    last = pe.transpose(val_ps[par][0:K, P * j:P * j + P], phi_sb[:, j, par, :], ident)
            last.then_inc(phi_turned, 1)
            keep_warm(1, bank[6])
            convolve_offsets(1)
            turn_offsets(1)
            pe.wait_ge(w_ready, 2)
            for m in range(5):
                rows = min(P, (TAPS - 2 * m) * C)
                last = pe.transpose(bank[6][0:rows, C * m:C * m + C], w_scaled[:, P * m:P * m + rows], ident[0:C, 0:C])
            last.then_inc(w_turned, 1)
            pe.wait_ge(off_laid, 2)
            pe.wait_ge(w_diag_ready, 1)
            pe.wait_ge(s_mats, 16 * 6 * BRANCHES)
            for r in range(BRANCHES):
                for par in range(2):
                    if r:
                        pe.wait_ge(mats_ready, 2 * r - 1 + par)
                    pe.matmul(bank[par][:], w_diag[:, r, 0, :], m_raw[:, r, 0].rearrange("d k e -> d (k e)"),
                              start=(r == 0), stop=False, skip_group_check=True)
                    pe.matmul(bank[par][:], w_diag[:, r, par, :], m_raw[:, r, 1].rearrange("d k e -> d (k e)"),
                              start=False, stop=(r == BRANCHES - 1), skip_group_check=True).then_inc(mats_summed, 1)
                if r:
                    pe.wait_ge(mu_ready, r)
                pe.matmul(bank[2][:, 0:3 * C], w_diag[:, r, 0, :], mu_raw[:, r, :], start=(r == 0),
                          stop=(r == BRANCHES - 1), skip_group_check=True).then_inc(mats_summed, 1)

            pe.wait_ge(diag_ready, 1)
            pe.matmul(bank[3][:, 0:K], ones[:], f_diag[:], start=True, stop=True).then_inc(f_scale_ready, 1)

            def turn_values(r):
                for b2 in range(2):
                    pe.wait_ge(v_ready[b2], START + r + 1)
                pe.wait_ge(y_used, START + r)
                for b2 in range(2):
                    for m in range(4):
                        pe.transpose(val_ps[b2][:, P * m:P * m + P], V[:, b2, P * m:P * m + P], ident)
                    last = pe.transpose(tail_ps[0:C, P * b2:P * b2 + P], V[:, b2, 4 * P:4 * P + C], ident)
                last.then_inc(val_turned, 1)

            def convolve_values(r):
                pe.wait_ge(val_copied, r + 1)
                pe.sem_inc(pe_marks, 1)
                for m in range(5):
                    rows = min(P, (TAPS - 2 * m) * C + 1)
                    for b2 in range(2):
                        last = pe.matmul(y_chan_ps[C * b2:C * b2 + C, :], w_main[0:rows, m, :], vT[0:rows, b2, m, :],
                                         start=(m == 0), stop=(m == 4))
                last.then_inc(y_convolved, 1)

            def turn_convolved(r):
                pe.wait_ge(y_copied, r + 1)
                pe.transpose(y_ps, y_chan[:], ident).then_inc(y_done, 1)

            def turn_tokens(r):
                pe.wait_ge(u_ready, r + 1)
                pe.wait_ge(u_copied, START + r)
                pe.matmul(tok_ps[:, 0:P], u_tok[:], swap, start=True, stop=True).then_inc(u_turned, 1)

            pe.wait_ge(w_copied, 1)
            pe.wait_ge(zeroed, 3)
            turn_values(0)
            convolve_values(0)
            turn_convolved(0)
            pe.wait_ge(mats_ready, 2 * BRANCHES)
            keep_warm(2, bank[0])
            turn_values(1)
            keep_warm(1, bank[0])
            convolve_values(1)
            turn_convolved(1)
            turn_tokens(0)
            keep_warm(WARM_UP_UNITS, bank[0])
            turn_tokens(1)

            for n in range(NQ):
                bp, j = divmod(n, NJ)
                seg0, nseg = unit_ranges(j)
                acc = acc_ps[n % 2]
                ranges = [(s, max(SEGS[s][0], P * j) - P * j, min(SEGS[s][1], P * j + P) - P * j)
                          for s in range(seg0, seg0 + nseg)]

                parts = ((u_hi, 0), (u_hi, 1), (u_lo, 0))

                def products(slot, b2):
                    dst = conv_ps[b2][:, 0:2 * NCOL].rearrange("c (t a) -> c t a", t=2)
                    for j2 in range(j + 1):
                        c0 = 1 + P * (j - j2)
                        for e, (u, part) in enumerate(parts):
                            last = pe.matmul(dst, u[:, NJ * bp + j2, b2].rearrange("s p c -> s (p c)"),
                                             ring_h[:, slot, :, part, c0:c0 + NCOL],
                                             start=(j2 == 0 and e == 0), stop=(j2 == j and e == 2))
                    return last

                def products_in_order(slot, b2):
                    for e, (u, part) in enumerate(parts):
                        for src in range(2):
                            h = ring_h[:, slot, src, part, 2 - src:2 - src + P]
                            h = bass.AP(h.tensor, h.offset, [h.ap[0], [(1, -1)[src] * 2 * HLEN + src, 2], [1, P]])
                            last = pe.matmul(conv_ps[b2][C * src:C * src + C, 0:2 * P].rearrange("c (p a) -> c p a", p=2),
                                             u[:, NJ * bp, b2, src], h, start=(e == 0), stop=(e == 2))
                    return last

                def convolve(kk, i):
                    slot = kk % NSLOT
                    pe.wait_ge(filt_loaded[slot], 32 * (4 * n + 2 * i + kk // NSLOT + 1))
                    for b2 in range(2):
                        pe.wait_ge(conv_copied[b2], START + 16 * n + 8 * i + kk)
                        (products if j else products_in_order)(slot, b2).then_inc(conv_done[b2], 1)

                def mix(kk, i):
                    slot = kk % NSLOT
                    for b2 in range(2):
                        pe.wait_ge(conv_copied[b2], START + 16 * n + 8 * i + kk + 1)
                    pe.sem_inc(pe_marks, 1)
                    for s, a0, a1 in ranges:
                        for p in range(2):
                            first = ((s - seg0) * 3 + p) * C
                            for b2 in range(2):
                                last = pe.matmul(acc[C * b2:C * b2 + C, P * p + a0:P * p + a1], ring_m[:, slot, first:first + C],
                                                 u_conv[:, kk % 2, b2, p, a0:a1], start=False, stop=False,
                                                 skip_group_check=True)
                    last.then_inc(filt_used[slot], 1)

                if n >= 2:
                    pe.wait_ge(out_copied, n - 1)
                pe.wait_ge(u_copied, START + 2 * n + 2)
                for p in range(2):
                    pe.matmul(acc[:, P * p:P * p + P], x2_tok[:, 2 * n + p].rearrange("s b c -> s (b c)"), swap,
                              start=(p == 0), stop=False, skip_group_check=True)
                for lag in range(3):
                    (src, shift), (src1, shift1) = [((p - lag) % 2, (p - lag) // 2) for p in range(2)]
                    for s, a0, a1 in ranges:
                        for b2 in range(2):
                            half = slice(C * b2, C * b2 + C)
                            u = uT[half, src, bp, 1 + P * j + shift + a0:1 + P * j + shift + a1]
                            u = bass.AP(u.tensor, u.offset, [u.ap[0], [(src1 - src) * BP * (1 + HALF) + shift1 - shift, 2], u.ap[-1]])
                            pe.matmul(acc[half, 0:2 * P].rearrange("e (p a) -> e p a", p=2)[:, :, a0:a1], mu[half, s, lag, :], u,
                                      start=False, stop=False, skip_group_check=True)
                with pe.Fori(0, 2) as i:
                    r = 2 * n + 2 + i
                    for kk in range(8):
                        convolve(kk, i)
                        if kk:
                            mix(kk - 1, i)
                        if n + 1 < NQ and kk == VALUES_AT:
                            turn_values(r)
                        if n + 1 < NQ and kk == Y_AT:
                            convolve_values(r)
                        if n + 1 < NQ and kk == Y_TURN_AT:
                            turn_convolved(r)
                        if n + 1 < NQ and kk == TOKENS_AT:
                            turn_tokens(r)
                    mix(7, i)


LINKS_PER_QUARTER = 61
VALUES_AT, Y_AT, Y_TURN_AT, TOKENS_AT = 0, 1, 2, 7


def unit_ranges(j):
    hit = [s for s, (a, b) in enumerate(SEGS) if a < P * (j + 1) and b > P * j]
    return hit[0], len(hit)


_INS = ['x', 'L0_conv_offset_w', 'L0_conv_offset_b', 'L0_conv_mask_w', 'L0_conv_mask_b', 'L0_conv_weight',
        'L0_conv_bn_gamma', 'L0_conv_bn_beta', 'L0_conv_bn_mean', 'L0_conv_bn_var', 'L0_ffn_sigma', 'L0_ffn_phi',
        'L0_ffn_M_u', 'L0_ffn_M_phi_plus', 'L0_ffn_M_phi_minus', 'L0_ffn_log_weights', 'L0_ffn_gumbel']


def constants():
    s = P - 1 - np.arange(P)
    grid = np.zeros((P, 2 * NJ, NOFF), np.float32)
    for j in range(NJ):
        for p in range(2):
            for t in range(TAPS):
                grid[:, 2 * j + p, 2 * t] = H + 1 - (8 * j + s // 16 + t // 3)
                grid[:, 2 * j + p, 2 * t + 1] = W + 1 - (2 * (s % 16) + p + t % 3)
    first = np.array([k % 2 * SIDE * SIDE for k in range(BLK)], np.float32)
    return {"ident": np.stack([np.eye(P), np.eye(P)[::-1], np.tile(np.eye(C), (2, 2))], 1).astype(np.float32), "grid": grid, "first_row": np.tile(first, (P, 1))}


def kernel(**inputs):
    import numpy as _np
    import concourse.bacc as _bacc
    from concourse import mybir as _mybir
    from concourse.bass_utils import run_bass_kernel_spmd as _run

    nc = _bacc.Bacc("TRN2", target_bir_lowering=False, num_devices=1)
    arrays, args = {}, []
    for name, a in [(n, inputs[n]) for n in _INS] + list(constants().items()):
        a = _np.ascontiguousarray(a)
        arrays[f"in_{name}_dram"] = a
        args.append(nc.dram_tensor(f"in_{name}_dram", a.shape, _mybir.dt.from_np(a.dtype), kind="ExternalInput").ap())
    args.append(nc.dram_tensor("out_0_dram", (B, C, H, W), _mybir.dt.float32, kind="ExternalOutput").ap())
    metaformer_kernel(nc, *args)
    r = _run(nc, [arrays], core_ids=[0])
    return r.results[0]["out_0_dram"]
```
